# Optimizing a Trainium2 kernel written in Bass

```python
import numpy as np
import jax
import jax.numpy as jnp

def _softmax(x, axis=-1):
    return jax.nn.softmax(x, axis=axis)

def _gelu(x):
    return jax.nn.gelu(x, approximate=True)

def _silu(x):
    return jax.nn.silu(x)

def _sigmoid(x):
    return jax.nn.sigmoid(x)

def _layernorm(x, axis=-1, eps=1e-05):
    m = jnp.mean(x, axis=axis, keepdims=True)
    v = jnp.var(x, axis=axis, keepdims=True)
    return (x - m) / jnp.sqrt(v + eps)

def _scatter_add(tgt, idx, src, axis=0):
    return tgt.at[idx].add(src)

def _segment_sum(src, seg, n):
    return jax.ops.segment_sum(src, seg, n)
kernel_name = 'mk_adj_resnorm_d4_adj_r2_2fde83'

def setup_inputs(seed: int=0):
    np.random.seed(seed)
    _w = jnp.asarray

    def _rec_inputs():
        import jax
        import jax.numpy as jnp
        _gk = jax.random.key(seed)
        x = 7.22e-05 + 1 * jax.random.normal(jax.random.fold_in(_gk, 1), (16, 512, 128), jnp.float32)
        _a = jax.random.bernoulli(jax.random.fold_in(_gk, 2), 0.00390625, (512, 512))
        _a = jnp.logical_or(_a, jnp.eye(512, dtype=bool))
        _af = _a.astype(jnp.float32)
        _af = _af * jax.random.uniform(jax.random.fold_in(_gk, 3), (512, 512), jnp.float32, 0.05, 1)
        adj = _af
        return (x, adj)
    x, adj = _rec_inputs()

    def _L0_gnn_setup():
        import jax, jax.numpy as jnp
        import numpy as np
        B, N, F_IN, F_OUT = (8, 4096, 128, 128)
        EPS = 1e-12
        key = jax.random.key(seed)
        k1, k2, k3, k4 = jax.random.split(key, 4)
        x = jax.random.normal(k1, (B, N, F_IN), dtype=jnp.float32)
        adj = jax.random.uniform(k2, (N, N), dtype=jnp.float32)
        weight = jax.random.normal(k3, (F_IN, F_OUT), dtype=jnp.float32) * 0.05
        bias = jax.random.normal(k4, (F_OUT,), dtype=jnp.float32) * 0.05
        return {'x': x, 'adj': adj, 'weight': weight, 'bias': bias}
    _L0_gnn_all = _L0_gnn_setup()
    _L0_gnn_in = {k: v for k, v in _L0_gnn_all.items() if k in ('weight', 'bias')}
    del _L0_gnn_all

    def _L1_gnn_setup():
        import jax, jax.numpy as jnp
        import numpy as np
        B, N, D = (32, 512, 128)
        TIME_STEP = 5
        key = jax.random.key(seed)
        ks = jax.random.split(key, 12)
        s2 = 1.0 / np.sqrt(2 * D)
        s1 = 1.0 / np.sqrt(D)
        return {'input': jax.random.normal(ks[0], (B, N, D), jnp.float32), 'in_matrix': jax.random.uniform(ks[1], (N, N), jnp.float32), 'out_matrix': jax.random.uniform(ks[2], (N, N), jnp.float32), 'w3_w': jax.random.normal(ks[3], (D, 2 * D), jnp.float32) * s2, 'w3_b': jnp.zeros((D,), jnp.float32), 'u3_w': jax.random.normal(ks[4], (D, D), jnp.float32) * s1, 'u3_b': jnp.zeros((D,), jnp.float32), 'w4_w': jax.random.normal(ks[5], (D, 2 * D), jnp.float32) * s2, 'w4_b': jnp.zeros((D,), jnp.float32), 'w5_w': jax.random.normal(ks[6], (D, 2 * D), jnp.float32) * s2, 'w5_b': jnp.zeros((D,), jnp.float32), 'u5_w': jax.random.normal(ks[7], (D, D), jnp.float32) * s1, 'u5_b': jnp.zeros((D,), jnp.float32), 'time_step': TIME_STEP}
    _L1_gnn_all = _L1_gnn_setup()
    _L1_gnn_in = {k: v for k, v in _L1_gnn_all.items() if k in ('w3_w', 'w3_b', 'u3_w', 'u3_b', 'w4_w', 'w4_b', 'w5_w', 'w5_b', 'u5_w', 'u5_b')}
    del _L1_gnn_all

    def _L2_gnn_setup():
        import jax, jax.numpy as jnp
        import numpy as np
        B, N, C_IN, C_OUT = (8, 1024, 128, 128)
        key = jax.random.key(seed)
        k1, k2, k3 = jax.random.split(key, 3)
        x = jax.random.normal(k1, (B, N, C_IN), dtype=jnp.float32)
        adj = jax.random.uniform(k2, (N, N), dtype=jnp.float32)
        W = jax.random.normal(k3, (C_OUT, C_IN), dtype=jnp.float32) * (1.0 / np.sqrt(C_IN))
        b = jnp.zeros((C_OUT,), dtype=jnp.float32)
        return {'x': x, 'adj': adj, 'W': W, 'b': b}
    _L2_gnn_all = _L2_gnn_setup()
    _L2_gnn_in = {k: v for k, v in _L2_gnn_all.items() if k in ('W', 'b')}
    del _L2_gnn_all

    def _L3_gnn_setup():
        import jax, jax.numpy as jnp
        import numpy as np
        NEG = -9000000000000000.0
        key = jax.random.key(seed)
        k1, k2, k3, k4 = jax.random.split(key, 4)
        B, N, F_in, F_out, MAX_E = (8192, 16, 128, 128, 128)
        inp = jax.random.normal(k1, (B, N, F_in), dtype=jnp.float32)
        adj = jax.random.uniform(k2, (N, N), dtype=jnp.float32)
        limit = 1.414 * np.sqrt(6.0 / (F_in + F_out))
        W = jax.random.uniform(k3, (2, F_in, F_out), dtype=jnp.float32, minval=-limit, maxval=limit)
        e = jnp.ones((1, MAX_E), dtype=jnp.float32)
        stdv = 1.0 / np.sqrt(F_out)
        bias = jax.random.uniform(k4, (F_out,), dtype=jnp.float32, minval=-stdv, maxval=stdv)
        return {'input': inp, 'adj': adj, 'W': W, 'e': e, 'bias': bias}
    _L3_gnn_all = _L3_gnn_setup()
    _L3_gnn_in = {k: v for k, v in _L3_gnn_all.items() if k in ('W', 'e', 'bias')}
    del _L3_gnn_all
    return {'x': x, 'adj': adj, 'L0_gnn_weight': _L0_gnn_in['weight'], 'L0_gnn_bias': _L0_gnn_in['bias'], 'L1_gnn_w3_w': _L1_gnn_in['w3_w'], 'L1_gnn_w3_b': _L1_gnn_in['w3_b'], 'L1_gnn_u3_w': _L1_gnn_in['u3_w'], 'L1_gnn_u3_b': _L1_gnn_in['u3_b'], 'L1_gnn_w4_w': _L1_gnn_in['w4_w'], 'L1_gnn_w4_b': _L1_gnn_in['w4_b'], 'L1_gnn_w5_w': _L1_gnn_in['w5_w'], 'L1_gnn_w5_b': _L1_gnn_in['w5_b'], 'L1_gnn_u5_w': _L1_gnn_in['u5_w'], 'L1_gnn_u5_b': _L1_gnn_in['u5_b'], 'L2_gnn_W': _L2_gnn_in['W'], 'L2_gnn_b': _L2_gnn_in['b'], 'L3_gnn_W': _L3_gnn_in['W'], 'L3_gnn_e': _L3_gnn_in['e'], 'L3_gnn_bias': _L3_gnn_in['bias']}

def reference(x, adj, L0_gnn_weight, L0_gnn_bias, L1_gnn_w3_w, L1_gnn_w3_b, L1_gnn_u3_w, L1_gnn_u3_b, L1_gnn_w4_w, L1_gnn_w4_b, L1_gnn_w5_w, L1_gnn_w5_b, L1_gnn_u5_w, L1_gnn_u5_b, L2_gnn_W, L2_gnn_b, L3_gnn_W, L3_gnn_e, L3_gnn_bias):
    import jax
    import jax.numpy as jnp

    def _L0_gnn_ref(x, adj, weight, bias):
        import jax, jax.numpy as jnp
        import numpy as np
        B, N, F_IN, F_OUT = (8, 4096, 128, 128)
        EPS = 1e-12
        y = jnp.einsum('nm,bmf->bnf', adj, x)
        y = y + x
        y = jnp.einsum('bnf,fo->bno', y, weight) + bias
        norm = jnp.sqrt(jnp.sum(y * y, axis=2, keepdims=True))
        y = y / jnp.maximum(norm, EPS)
        return y

    def _L1_gnn_ref(input, in_matrix, out_matrix, w3_w, w3_b, u3_w, u3_b, w4_w, w4_b, w5_w, w5_b, u5_w, u5_b, time_step):
        import jax, jax.numpy as jnp
        import numpy as np
        B, N, D = (32, 512, 128)
        TIME_STEP = 5

        def step(h, _):
            m_in = jnp.einsum('nm,bmd->bnd', in_matrix, h)
            m_out = jnp.einsum('nm,bmd->bnd', out_matrix, h)
            av = jnp.concatenate([m_in, m_out], axis=-1)
            u3 = h @ u3_w.T + u3_b
            z = jax.nn.sigmoid(av @ w3_w.T + w3_b + u3)
            r = jax.nn.sigmoid(av @ w4_w.T + w4_b + u3)
            hv = jnp.tanh(av @ w5_w.T + w5_b + (r * h @ u5_w.T + u5_b))
            h = (1.0 - z) * h + z * hv
            return (h, None)
        h, _ = jax.lax.scan(step, input, None, length=time_step)
        return h

    def _L2_gnn_ref(x, adj, W, b):
        import jax, jax.numpy as jnp
        import numpy as np
        B, N, C_IN, C_OUT = (8, 1024, 128, 128)
        n = x.shape[1]
        A_hat = adj + jnp.eye(n, dtype=adj.dtype)
        d = jnp.sum(A_hat, axis=-1) ** (-0.5)
        A_norm = d[:, None] * A_hat * d[None, :]
        out = jnp.einsum('nm,bmc->bnc', A_norm, x)
        out = jnp.einsum('bnc,oc->bno', out, W) + b
        return out

    def _L3_gnn_ref(input, adj, W, e, bias):
        import jax, jax.numpy as jnp
        import numpy as np
        NEG = -9000000000000000.0
        h0 = jnp.einsum('bnf,fg->bng', input, W[0])
        h1 = jnp.einsum('bnf,fg->bng', input, W[1])
        m = adj > 0
        idx = jnp.cumsum(m.reshape(-1).astype(jnp.int32)) - 1
        vals = e[0][idx].reshape(adj.shape)
        A = jnp.where(m, vals, jnp.float32(NEG))
        A = jax.nn.softmax(A, axis=1)
        M = jnp.eye(adj.shape[0], dtype=A.dtype)
        out = jnp.einsum('ij,bjg->big', A * M, h0) + jnp.einsum('ij,bjg->big', A * (1.0 - M), h1)
        return out + bias[None, None, :]
    x = _layernorm(x + _L0_gnn_ref(x, adj, L0_gnn_weight, L0_gnn_bias), axis=-1)
    x = _layernorm(x + _L1_gnn_ref(x, adj, adj, L1_gnn_w3_w, L1_gnn_w3_b, L1_gnn_u3_w, L1_gnn_u3_b, L1_gnn_w4_w, L1_gnn_w4_b, L1_gnn_w5_w, L1_gnn_w5_b, L1_gnn_u5_w, L1_gnn_u5_b, 5), axis=-1)
    x = _layernorm(x + _L2_gnn_ref(x, adj, L2_gnn_W, L2_gnn_b), axis=-1)
    x = _layernorm(x + _L3_gnn_ref(x, adj, L3_gnn_W, L3_gnn_e, L3_gnn_bias), axis=-1)
    return x

_drawn_inputs = setup_inputs


def setup_inputs(seed=0):
    import zlib

    import numpy as np

    out = dict(_drawn_inputs(seed))
    spreads = {'L1_gnn_w3_b': (0.0, 0.33),
     'L1_gnn_u3_b': (0.0, 0.295),
     'L1_gnn_w4_b': (0.0, 0.8),
     'L1_gnn_w5_b': (0.0, 0.1),
     'L1_gnn_u5_b': (0.0, 0.1),
     'L2_gnn_b': (0.0, 0.1),
     'L3_gnn_e': (1.0, 0.6)}
    factors = {'L0_gnn_bias': 7.12}
    for name, (base, spread) in spreads.items():
        noise = np.random.default_rng([zlib.crc32(name.encode()), seed]).standard_normal(out[name].shape)
        drawn = base * np.exp(spread * noise) if base else spread * noise
        out[name] = jnp.asarray(drawn.astype(out[name].dtype))
    for name, factor in factors.items():
        out[name] = (out[name] * factor).astype(out[name].dtype)
    return out
```

```python
from contextlib import ExitStack

import concourse.bass as bass
from concourse import mybir

P = 128
B, N, D = 16, 512, 128
T = N // P
STEPS = 5
EPS_NORM, EPS_LN = 1e-12, 1e-5
NEG = -9000000000000000.0
F32 = mybir.dt.float32
F32R = mybir.dt.float32r
I32 = mybir.dt.int32
ALU = mybir.AluOpType
ACT = mybir.ActivationFunctionType
AX = mybir.AxisListType

L0, L2, L3 = 0, STEPS + 1, STEPS + 2
UNITS = B * (STEPS + 3)
LAST = B * STEPS
AFTER = B * (STEPS + 1)
LOOP_FROM = B + 6
LOOPS = STEPS - 1
MIX_AT = AFTER - 10


def stage(u):
    return u // B


def is_step(u):
    return B <= u < AFTER


def is_inner(u):
    return B <= u < LAST


STATE_LAG = 6


def turn_lag(u):
    return STATE_LAG if is_inner(u) else 7 if is_step(u) else 2


def has_norm(u):
    return 0 <= u < UNITS and not is_inner(u)


def is_turned_back(u):
    return 0 <= u < UNITS and stage(u) in (L0, L2)


SLOTS = UNITS + 6
NORMED = sorted((u for u in range(UNITS) if has_norm(u)), key=lambda u: (u + turn_lag(u), -u))
SPLIT = [u for u in NORMED if stage(u) != L3]
BACK = [u for u in NORMED if is_turned_back(u)]


def norms_at(s, lag):
    return [u for u in NORMED if u + turn_lag(u) + lag == s]


def turns_at(s):
    found = []
    if is_inner(s - STATE_LAG):
        found.append(("state", s - STATE_LAG))
    found += [("result", u) for u in norms_at(s, 0)]
    found += [("back", u) for u in norms_at(s, 3) if is_turned_back(u)]
    if MIX_AT <= s < MIX_AT + T:
        found.append(("mix", s - MIX_AT))
    if s == MIX_AT + T + 2:
        found.append(("diagonal", 0))
    return found


TURNS = [x for s in range(SLOTS) for x in turns_at(s)]
TURN_NO = {x: i for i, x in enumerate(TURNS)}


def graph_layers(nc, x, adj, w0, b0, w3, b3, u3, ub3, w4, b4, w5, b5, u5, ub5, w2, b2, wl3, e, bl3, out):
    with ExitStack() as ctx:
        def sb(name, shape, dt=F32):
            return ctx.enter_context(nc.sbuf_tensor(name, shape, dt))

        def sem(name):
            return ctx.enter_context(nc.semaphore(name))

        def bank(name):
            return ctx.enter_context(nc.psum_tensor(name, [P, N], F32))

        res = sb("res", [P, B, T, D])
        nat_hi = sb("nat_hi", [P, B, T, D], F32R)
        nat_lo = sb("nat_lo", [P, B, T, D], F32R)
        feat = sb("feat", [P, B, N])
        adj_hi = sb("adj_hi", [P, T, N], F32R)
        adj_lo = sb("adj_lo", [P, T, N], F32R)
        eye_hi = sb("eye_hi", [P, T, N], F32R)
        eye_lo = sb("eye_lo", [P, T, N], F32R)
        later = sb("later", [P, T, N])
        rows = sb("rows", [P, T, N])
        agg_hi = sb("agg_hi", [P, 2, N], F32R)
        agg_lo = sb("agg_lo", [P, 2, N], F32R)
        gate_r = sb("gate_r", [P, 2, N])
        gate_z = sb("gate_z", [P, 2, N])
        cand = sb("cand", [P, 2, N])
        W_R, W_ZR, W_H, W_L0, W_L2, W_L3 = range(6)
        w_hi = sb("w_hi", [P, 6, D], F32R)
        w_lo = sb("w_lo", [P, 6, D], F32R)
        U_GATE, U_CAND, U_SELF = range(3)
        w_full = sb("w_full", [P, 3, D])
        ident = sb("ident", [P, P])
        B_L0, B_R, B_Z, B_H, B_L2, B_L3 = range(6)
        bias = sb("bias", [P, 6])
        eps = sb("eps", [P, 1])
        sumsq = sb("sumsq", [P, 4, T])
        stats = sb("stats", [P, 4, T, 6])
        mean_var = sb("mean_var", [P, 4, T, 2])
        std = sb("std", [P, 4, T])
        e_last = sb("e_last", [P, 1])
        e_col = sb("e_col", [P, 1])
        small = sb("small", [P, 8, T])

        mask, count, chosen, value = (feat[:, 4 * i:4 * i + 4, :] for i in range(4))
        raw = gate_z[:, :, :].rearrange("p a n -> p (a n)")
        RAW_W3, RAW_W4, RAW_W5, RAW_U3, RAW_U5, RAW_W2 = 0, 256, 512, 768, 896, None
        raw2 = cand[:, 0, 0:D]
        raw0 = cand[:, 0, D:2 * D]
        rawl3 = cand[:, 0, 2 * D:3 * D]
        folded = cand[:, 1, 0:3 * D].rearrange("p (a d) -> p a d", a=3)
        bias_raw = cand[:, 1, 3 * D:3 * D + 10]
        tri = gate_r[:, 0, 0:P]
        ones = gate_r[:, 0, P:2 * P]
        kk = gate_r[:, 0, 2 * P:3 * P]
        owner = gate_r[:, 0, 3 * P:4 * P]
        owner_t = gate_r[:, 1, 0:P]
        kcol = gate_r[:, 1, P:P + 1]
        kk_int = gate_r[:, 1, 2 * P:3 * P].bitcast(I32)
        kcol_int = gate_r[:, 1, 3 * P:3 * P + 1].bitcast(I32)
        before = gate_r[:, 1, P + 1:P + 2]
        upto = gate_r[:, 1, P + 2:P + 3]
        diag_d = value[:, 0, :].rearrange("p (t q) -> p t q", t=T)
        d_row = value[:, 1, :]
        diag_m = rows[:, 0, :].rearrange("p (t q) -> p t q", t=T)
        diag_row = rows[:, 1, :]
        ones_late = rows[:, 2, 0:P]
        ident_off = rows[:, 2, P:2 * P]
        diag_junk = rows[:, 3, :].rearrange("p (t q) -> p t q", t=T)
        diag_col = small[:, 6, :]
        square_out = cand[:, 1, 0:D]

        agg_ps = [bank(f"agg_ps{i}") for i in range(2)]
        gate_ps = [bank(f"gate_ps{i}") for i in range(2)]
        cand_ps = [bank(f"cand_ps{i}") for i in range(2)]
        turn_ps = [bank(f"turn_ps{i}") for i in range(2)]
        prep_ps = agg_ps + gate_ps

        adj_in, param_in, stored = sem("adj_in"), sem("param_in"), sem("stored")
        x_in = [sem(f"x_in{b}") for b in range(B)]
        const_made = sem("const_made")
        folded_made = sem("folded_made")
        w_turned = sem("w_turned")
        w_hi_made, w_lo_made = sem("w_hi_made"), sem("w_lo_made")
        adj_turned, adj_hi_made, adj_lo_made = sem("adj_turned"), sem("adj_hi_made"), sem("adj_lo_made")
        prep_dve, prep_pe, prep_act = sem("prep_dve"), sem("prep_pe"), sem("prep_act")
        eye_hi_made, eye_lo_made = sem("eye_hi_made"), sem("eye_lo_made")
        x_hi_made, x_lo_made = sem("x_hi_made"), sem("x_lo_made")
        agg_done, agg_hi_made, agg_lo_made = sem("agg_done"), sem("agg_hi_made"), sem("agg_lo_made")
        gate_done = sem("gate_done")
        z_done, cand_done = sem("z_done"), sem("cand_done")
        r_made, y_made = sem("r_made"), sem("y_made")
        reset_made = sem("reset_made")
        z_made, cand_made = sem("z_made"), sem("cand_made")
        diff_made, move_made, state_made = sem("diff_made"), sem("move_made"), sem("state_made")
        turned, turn_read = sem("turned"), sem("turn_read")
        state_hi_made = sem("state_hi_made")
        sumsq_made, length_made = sem("sumsq_made"), sem("length_made")
        norm_dve = sem("norm_dve")
        stats_made, std_made, normed = sem("stats_made"), sem("std_made"), sem("normed")
        split_hi_made, split_lo_made = sem("split_hi_made"), sem("split_lo_made")
        norm2_hi_made, norm2_lo_made = sem("norm2_hi_made"), sem("norm2_lo_made")
        mix_dve = sem("mix_dve")
        mix_hi_made, mix_lo_made = sem("mix_hi_made"), sem("mix_lo_made")

        def count_of(order, u):
            return order.index(u) + 1

        def rows_ready(eng, u, ahead):
            if u < B:
                eng.wait_ge(x_hi_made, u + 1)
                eng.wait_ge(x_lo_made, u + 1)
            elif B * 2 <= u < AFTER:
                eng.wait_ge(state_hi_made, ahead(u - 2 * B + 1))
                eng.wait_ge(turn_read, ahead(TURN_NO["state", u - B] + 1))
            else:
                eng.wait_ge(split_hi_made, count_of(SPLIT, u - B))
                eng.wait_ge(split_lo_made, count_of(SPLIT, u - B))

        def run(eng, slot):
            for s in range(LOOP_FROM):
                slot(s, lambda v: v)
            with eng.Fori(0, LOOPS * B, B) as done:
                for s in range(LOOP_FROM, LOOP_FROM + B):
                    slot(s, lambda v: v + done)
            for s in range(LOOP_FROM + LOOPS * B, SLOTS):
                slot(s, lambda v: v)

        block = ctx.enter_context(nc.Block())

        @block.sync
        def _(sp):
            sp.dma_start(rows[:, :, :], adj.rearrange("(p t) m -> p t m", t=T)).then_inc(adj_in, 16)
            for b in range(B):
                sp.dma_start(res[:, b, :, :], x[b].rearrange("(p t) d -> p t d", t=T)).then_inc(x_in[b], 16)
            for u in range(UNITS - B, UNITS):
                sp.wait_ge(normed, count_of(NORMED, u))
                sp.dma_start(out[u % B].rearrange("(p t) d -> p t d", t=T), res[:, u % B, :, :]).then_inc(stored, 16)
            sp.wait_ge(stored, 16 * B)

        @block.scalar
        def _(act):
            def col(v):
                return v.rearrange("(d o) -> d o", o=1)

            for src, at in ((w3, RAW_W3), (w4, RAW_W4), (w5, RAW_W5)):
                act.dma_start(raw[:, at:at + 2 * D], src).then_inc(param_in, 16)
            act.dma_start(raw[:, RAW_U3:RAW_U3 + D], u3).then_inc(param_in, 16)
            act.dma_start(raw[:, RAW_U5:RAW_U5 + D], u5).then_inc(param_in, 16)
            act.dma_start(raw2, w2).then_inc(param_in, 16)
            act.dma_start(raw0, w0).then_inc(param_in, 16)
            act.dma_start(w_full[:, U_SELF, :], wl3[0]).then_inc(param_in, 16)
            act.dma_start(rawl3, wl3[1]).then_inc(param_in, 16)
            act.dma_start(bias[:, B_L0:B_L0 + 1], col(b0)).then_inc(param_in, 16)
            act.dma_start(bias[:, B_L2:B_L2 + 1], col(b2)).then_inc(param_in, 16)
            act.dma_start(bias[:, B_L3:B_L3 + 1], col(bl3)).then_inc(param_in, 16)
            for i, v in enumerate((b3, b4, b5, ub3, ub5)):
                act.dma_start(bias_raw[:, i:i + 1], col(v)).then_inc(param_in, 16)
            act.dma_start(e_col[:, :], e.rearrange("o k -> k o")).then_inc(param_in, 16)
            act.dma_start(e_last[:, :], e[0:1, P - 1:P].to_broadcast([P, 1])).then_inc(param_in, 16)

            act.wait_ge(param_in, 16 * 19)
            act.activation(w_hi[:, W_L0, :], raw0, ACT.Copy)
            act.activation(w_hi[:, W_L3, :], rawl3, ACT.Copy)
            act.wait_ge(w_turned, 1)
            act.activation(w_hi[:, W_R:W_H + 1, :], cand_ps[0][:, 0:3 * D].rearrange("p (a d) -> p a d", a=3), ACT.Copy)
            act.activation(w_hi[:, W_L2, :], cand_ps[0][:, 3 * D:4 * D], ACT.Copy).then_inc(w_hi_made, 1)
            for k in range(T):
                act.wait_ge(adj_turned, k + 1)
                act.activation(adj_hi[:, k, :], prep_ps[k][:, :], ACT.Copy).then_inc(adj_hi_made, 1)
            act.wait_ge(prep_dve, STEP_EYE)
            act.activation(eye_hi[:, :, :], later[:, :, :], ACT.Copy).then_inc(eye_hi_made, 1)
            act.wait_ge(prep_dve, STEP_ROWSUM)
            act.activation(small[:, 1, :], small[:, 0, :], ACT.Sqrt).then_inc(prep_act, 1)
            act.wait_ge(prep_dve, STEP_NEGMAX)
            for t in range(T):
                act.activation(rows[:, t, :], mask[:, t, :], ACT.Exp, bias=small[:, 3, t:t + 1],
                               accum_out=small[:, 4, t:t + 1]).then_inc(prep_act, 1)
            for b in range(B):
                act.wait_ge(x_in[b], 16)
                act.activation(nat_hi[:, b, :, :], res[:, b, :, :], ACT.Copy).then_inc(x_hi_made, 1)

            def slot(s, ahead):
                u = s - 2
                if is_step(u):
                    act.wait_ge(z_done, ahead(u - B + 1))
                    if u >= B + 2:
                        act.wait_ge(move_made, ahead(u - B - 1))
                    act.activation(gate_z[:, u % 2, :], gate_ps[u % 2][:, :], ACT.Sigmoid,
                                   bias=bias[:, B_Z:B_Z + 1]).then_inc(z_made, 1)
                for n in norms_at(s, 1):
                    i = NORMED.index(n)
                    act.wait_ge(stats_made, i + 1)
                    act.activation(std[:, i % 4, :], mean_var[:, i % 4, :, 1], ACT.Sqrt,
                                   bias=eps[:, 0:1]).then_inc(std_made, 1)
                for n in norms_at(s, 3):
                    if stage(n) != L3:
                        act.wait_ge(normed, count_of(NORMED, n))
                        act.activation(nat_hi[:, n % B, :, :], res[:, n % B, :, :], ACT.Copy).then_inc(split_hi_made, 1)
                if s < UNITS:
                    act.wait_ge(agg_done, ahead(s + 1))
                    if s >= 2:
                        act.wait_ge(gate_done, ahead(s - 1))
                    if B + 2 <= s < AFTER + 2:
                        act.wait_ge(z_done, ahead(s - 2 - B + 1))
                    act.activation(agg_hi[:, s % 2, :], agg_ps[s % 2][:, :], ACT.Copy).then_inc(agg_hi_made, 1)
                u = s - 1
                if is_step(u):
                    act.wait_ge(gate_done, ahead(u + 1))
                    if u >= B + 2:
                        act.wait_ge(cand_done, ahead(u - B - 1))
                    elif u >= 2:
                        act.wait_ge(turned, TURN_NO["result", u - 2] + 1)
                    act.activation(gate_r[:, u % 2, :], gate_ps[u % 2][:, :], ACT.Sigmoid,
                                   bias=bias[:, B_R:B_R + 1]).then_inc(r_made, 1)
                elif 0 <= u < UNITS:
                    act.wait_ge(gate_done, u + 1)
                    if is_step(u - 2):
                        act.wait_ge(cand_done, u - 2 - B + 1)
                    elif u >= 2:
                        act.wait_ge(turned, TURN_NO["result", u - 2] + 1)
                    at = {L0: B_L0, L2: B_L2, L3: B_L3}[stage(u)]
                    act.activation(gate_r[:, u % 2, :], gate_ps[u % 2][:, :], ACT.Identity,
                                   bias=bias[:, at:at + 1]).then_inc(y_made, 1)
                u = s - 2
                if is_step(u):
                    act.wait_ge(cand_done, ahead(u - B + 1))
                    if u >= B + 2:
                        act.wait_ge(state_made, ahead(u - B - 1))
                    act.activation(cand[:, u % 2, :], cand_ps[u % 2][:, :], ACT.Tanh,
                                   bias=bias[:, B_H:B_H + 1]).then_inc(cand_made, 1)
                u = s - STATE_LAG
                if is_inner(u):
                    k = TURN_NO["state", u]
                    act.wait_ge(turned, ahead(k + 1))
                    act.activation(nat_hi[:, u % B, :, :], turn_ps[k % 2][:, :].rearrange("p (t d) -> p t d", t=T),
                                   ACT.Copy).then_inc(state_hi_made, 1)
                for n in norms_at(s, 0):
                    if stage(n) == L0:
                        k, i = TURN_NO["result", n], NORMED.index(n)
                        act.wait_ge(turned, k + 1)
                        for t in range(T):
                            last = act.activation(square_out[:, :], turn_ps[k % 2][:, t * D:(t + 1) * D],
                                                  ACT.Square, accum_out=sumsq[:, i % 4, t:t + 1])
                            last.then_inc(sumsq_made, 1)
                            act.wait_ge(sumsq_made, T * i + t + 1)
                        act.activation(sumsq[:, i % 4, :], sumsq[:, i % 4, :], ACT.Sqrt).then_inc(length_made, 1)
                k = s - (B + 1)
                if 0 <= k < T:
                    act.wait_ge(agg_done, B)
                    act.activation(eye_hi[:, k, :], later[:, k, :], ACT.Copy).then_inc(norm2_hi_made, 1)
                k = s - AFTER
                if 0 <= k < T:
                    if k == 0:
                        act.wait_ge(agg_done, AFTER)
                        act.wait_ge(mix_dve, MIX_READY)
                    act.activation(adj_hi[:, k, :], later[:, k, :], ACT.Copy).then_inc(mix_hi_made, 1)

            run(act, slot)

        @block.gpsimd
        def _(pool):
            pool.memset(ident[:, :], 1.0).then_inc(const_made, 1)
            pool.memset(tri, 1.0).then_inc(const_made, 1)
            pool.memset(ones, 1.0).then_inc(const_made, 1)
            pool.memset(eps[:, :], EPS_LN).then_inc(const_made, 1)
            pool.iota(kk_int, [[1, P]], base=1, channel_multiplier=0).then_inc(const_made, 1)
            pool.iota(kcol_int, [[1, 1]], base=1, channel_multiplier=1).then_inc(const_made, 1)
            pool.wait_ge(const_made, 2)
            pool.affine_select(ident[:, :], ident[:, :], pattern=[[-1, P]], compare_op=ALU.is_equal, fill=0.0,
                               base=0, channel_multiplier=1).then_inc(const_made, 1)
            pool.affine_select(tri, tri, pattern=[[1, P]], compare_op=ALU.is_gt, fill=0.0,
                               base=0, channel_multiplier=-1).then_inc(const_made, 1)
            for b in range(B):
                pool.wait_ge(x_hi_made, b + 1)
                pool.tensor_tensor(nat_lo[:, b, :, :], res[:, b, :, :], nat_hi[:, b, :, :].bitcast(F32),
                                   ALU.subtract).then_inc(x_lo_made, 1)
            for i, n in enumerate(SPLIT):
                pool.wait_ge(split_hi_made, i + 1)
                pool.tensor_tensor(nat_lo[:, n % B, :, :], res[:, n % B, :, :], nat_hi[:, n % B, :, :].bitcast(F32),
                                   ALU.subtract).then_inc(split_lo_made, 1)

        @block.vector
        def _(dve):
            done = [0]

            def link(ins):
                done[0] += 1
                ins.then_inc(prep_dve, 1)
                dve.wait_ge(prep_dve, done[0])

            dve.wait_ge(param_in, 16 * 19)
            half = lambda at: (raw[:, at:at + D], raw[:, at + D:at + 2 * D])
            link(dve.tensor_tensor(folded[:, 0, :], *half(RAW_W4), ALU.add))
            link(dve.tensor_tensor(folded[:, 1, :], *half(RAW_W3), ALU.add))
            link(dve.tensor_tensor(folded[:, 2, :], *half(RAW_W5), ALU.add))
            link(dve.tensor_tensor(folded[:, 1, :], folded[:, 1, :], folded[:, 0, :], ALU.subtract))
            link(dve.tensor_tensor(bias[:, B_R:B_R + 1], bias_raw[:, 1:2], bias_raw[:, 3:4], ALU.add))
            link(dve.tensor_tensor(bias[:, B_Z:B_Z + 1], bias_raw[:, 0:1], bias_raw[:, 3:4], ALU.add))
            link(dve.tensor_tensor(bias[:, B_H:B_H + 1], bias_raw[:, 2:3], bias_raw[:, 4:5], ALU.add))
            assert done[0] == STEP_FOLDED
            dve.wait_ge(w_hi_made, 1)
            link(dve.tensor_tensor(w_lo[:, W_L0, :], raw0, w_hi[:, W_L0, :].bitcast(F32), ALU.subtract))
            link(dve.tensor_tensor(w_lo[:, W_L3, :], rawl3, w_hi[:, W_L3, :].bitcast(F32), ALU.subtract))
            link(dve.tensor_tensor(w_lo[:, W_R:W_H + 1, :], cand_ps[0][:, 0:3 * D].rearrange("p (a d) -> p a d", a=3),
                                   w_hi[:, W_R:W_H + 1, :].bitcast(F32), ALU.subtract))
            link(dve.tensor_tensor(w_lo[:, W_L2, :], cand_ps[0][:, 3 * D:4 * D], w_hi[:, W_L2, :].bitcast(F32), ALU.subtract))
            link(dve.tensor_copy(w_full[:, 0:2, :], cand_ps[1][:, 0:2 * D].rearrange("p (a d) -> p a d", a=2)))
            assert done[0] == STEP_WEIGHTS
            for k in range(T):
                dve.wait_ge(adj_hi_made, k + 1)
                dve.tensor_tensor(adj_lo[:, k, :], prep_ps[k][:, :], adj_hi[:, k, :].bitcast(F32),
                                  ALU.subtract).then_inc(adj_lo_made, 1)
                link(dve.tensor_copy(later[:, k, :], prep_ps[k][:, :]))
            for k in range(T):
                diag = later[:, k, k * P:(k + 1) * P]
                link(dve.tensor_tensor(diag, diag, ident[:, :], ALU.add))
            assert done[0] == STEP_EYE
            dve.wait_ge(eye_hi_made, 1)
            link(dve.tensor_tensor(eye_lo[:, :, :], later[:, :, :], eye_hi[:, :, :].bitcast(F32), ALU.subtract))
            link(dve.tensor_reduce(small[:, 0, :], rows[:, :, :], AX.X, ALU.add))
            link(dve.tensor_scalar(small[:, 0, :], small[:, 0, :], 1.0, None, ALU.add))
            assert done[0] == STEP_ROWSUM
            dve.wait_ge(prep_act, 1)
            link(dve.reciprocal(small[:, 2, :], small[:, 1, :]))
            for t in range(T):
                link(dve.tensor_scalar(diag_d[:, t, :], ident[:, :], small[:, 2, t:t + 1], None, ALU.mult))
            assert done[0] == STEP_DIAG
            dve.wait_ge(prep_pe, PE_DROW)
            link(dve.tensor_copy(d_row, cand_ps[1][:, :]))
            for k in range(T):
                link(dve.scalar_tensor_tensor(out=later[:, k, :], in0=later[:, k, :], scalar=small[:, 2, k:k + 1],
                                              in1=d_row, op0=ALU.mult, op1=ALU.mult))
            link(dve.tensor_copy(kk, kk_int))
            link(dve.tensor_copy(kcol, kcol_int))
            flat = lambda v: v.rearrange("p a n -> p (a n)")
            link(dve.tensor_scalar(mask, rows[:, :, :], 0.0, None, ALU.is_gt))
            link(dve.tensor_tensor_scan(flat(count), flat(mask), flat(mask), 0.0, ALU.add, ALU.max))
            assert done[0] == STEP_SCAN
            dve.wait_ge(prep_pe, PE_BEFORE)
            link(dve.tensor_copy(before, cand_ps[0][:, 0:1]))
            link(dve.tensor_tensor(upto, before, count[:, T - 1, N - 1:N], ALU.add))
            link(dve.scalar_tensor_tensor(out=flat(count), in0=flat(count), scalar=before, in1=flat(mask),
                                          op0=ALU.add, op1=ALU.mult))
            link(dve.tensor_scalar(owner, kk, before, None, ALU.is_gt))
            link(dve.scalar_tensor_tensor(out=owner, in0=kk, scalar=upto, in1=owner, op0=ALU.is_le, op1=ALU.mult))
            assert done[0] == STEP_OWNER
            dve.wait_ge(prep_pe, PE_OWNER)
            link(dve.tensor_copy(owner_t, cand_ps[1][:, 0:P]))
            for k in range(T):
                dve.wait_ge(prep_pe, PE_CHOSEN + k)
                link(dve.tensor_scalar(chosen[:, k, :], prep_ps[k][:, :], kcol, e_col[:, 0:1], ALU.is_equal, ALU.mult))
            assert done[0] == STEP_CHOSEN
            link(dve.tensor_scalar(value, count, float(P), e_last[:, 0:1], ALU.is_gt, ALU.mult))
            link(dve.tensor_scalar(mask, mask, -NEG, NEG, ALU.mult, ALU.add))
            link(dve.tensor_tensor(mask, mask, value, ALU.add))
            for k in range(T):
                dve.wait_ge(prep_pe, PE_VALUE + k)
                link(dve.tensor_tensor(mask[:, k, :], mask[:, k, :], prep_ps[k][:, :], ALU.add))
            link(dve.tensor_reduce(small[:, 3, :], mask, AX.X, ALU.max))
            link(dve.tensor_scalar(small[:, 3, :], small[:, 3, :], -1.0, None, ALU.mult))
            assert done[0] == STEP_NEGMAX
            dve.wait_ge(prep_act, 1 + T)
            link(dve.reciprocal(small[:, 5, :], small[:, 4, :]))
            for t in range(T):
                link(dve.tensor_scalar(rows[:, t, :], rows[:, t, :], small[:, 5, t:t + 1], None, ALU.mult))
            assert done[0] == STEP_PREP

            norm_steps = [0]

            def norm_link(ins):
                norm_steps[0] += 1
                ins.then_inc(norm_dve, 1)
                dve.wait_ge(norm_dve, norm_steps[0])

            mix_steps = [0]

            def mix_link(ins):
                mix_steps[0] += 1
                ins.then_inc(mix_dve, 1)
                dve.wait_ge(mix_dve, mix_steps[0])

            def slot(s, ahead):
                for n in norms_at(s, 1):
                    k, i, b = TURN_NO["result", n], NORMED.index(n), n % B
                    dve.wait_ge(turned, k + 1)
                    if stage(n) == L0:
                        dve.wait_ge(length_made, i + 1)
                        norm_link(dve.tensor_scalar(sumsq[:, i % 4, :], sumsq[:, i % 4, :], EPS_NORM, None, ALU.max))
                        norm_link(dve.reciprocal(sumsq[:, i % 4, :], sumsq[:, i % 4, :]))
                        for t in range(T):
                            last = dve.scalar_tensor_tensor(
                                out=res[:, b, t, :], in0=turn_ps[k % 2][:, t * D:(t + 1) * D],
                                scalar=sumsq[:, i % 4, t:t + 1], in1=res[:, b, t, :], op0=ALU.mult, op1=ALU.add)
                        last.then_inc(turn_read, 1)
                    else:
                        dve.tensor_tensor(res[:, b, :, :], turn_ps[k % 2][:, :].rearrange("p (t d) -> p t d", t=T),
                                          res[:, b, :, :], ALU.add).then_inc(turn_read, 1)
                    dve.wait_ge(turn_read, k + 1)
                    for t in range(T):
                        last = dve.bn_stats(stats[:, i % 4, t, :], res[:, b, t, :])
                    norm_link(last)
                    for t in range(T):
                        last = dve.bn_aggr(mean_var[:, i % 4, t, :], stats[:, i % 4, t, :])
                    last.then_inc(stats_made, 1)
                for n in norms_at(s, 4):
                    if is_turned_back(n):
                        k = TURN_NO["back", n]
                        dve.wait_ge(turned, k + 1)
                        if stage(n) == L0:
                            dve.tensor_copy(feat[:, n % B, :], turn_ps[k % 2][:, :]).then_inc(turn_read, 1)
                        else:
                            dve.tensor_tensor(feat[:, n % B, :], turn_ps[k % 2][:, :], diag_row,
                                              ALU.mult).then_inc(turn_read, 1)
                if s < UNITS:
                    dve.wait_ge(agg_hi_made, ahead(s + 1))
                    dve.tensor_tensor(agg_lo[:, s % 2, :], agg_ps[s % 2][:, :], agg_hi[:, s % 2, :].bitcast(F32),
                                      ALU.subtract).then_inc(agg_lo_made, 1)
                u = s - 1
                if is_step(u):
                    dve.wait_ge(r_made, ahead(u - B + 1))
                    dve.tensor_tensor(gate_r[:, u % 2, :], gate_r[:, u % 2, :], feat[:, u % B, :],
                                      ALU.mult).then_inc(reset_made, 1)
                u = s - 2
                if is_step(u):
                    dve.wait_ge(cand_made, ahead(u - B + 1))
                    dve.tensor_tensor(cand[:, u % 2, :], cand[:, u % 2, :], feat[:, u % B, :],
                                      ALU.subtract).then_inc(diff_made, 1)
                    dve.wait_ge(diff_made, ahead(u - B + 1))
                    dve.wait_ge(z_made, ahead(u - B + 1))
                    dve.tensor_tensor(cand[:, u % 2, :], cand[:, u % 2, :], gate_z[:, u % 2, :],
                                      ALU.mult).then_inc(move_made, 1)
                    dve.wait_ge(move_made, ahead(u - B + 1))
                    dve.tensor_tensor(feat[:, u % B, :], feat[:, u % B, :], cand[:, u % 2, :],
                                      ALU.add).then_inc(state_made, 1)
                for n in norms_at(s, 2):
                    i, b = NORMED.index(n), n % B
                    dve.wait_ge(std_made, i + 1)
                    norm_link(dve.reciprocal(std[:, i % 4, :], std[:, i % 4, :]))
                    for t in range(T):
                        last = dve.tensor_scalar(res[:, b, t, :], res[:, b, t, :], mean_var[:, i % 4, t, 0:1],
                                                 std[:, i % 4, t:t + 1], ALU.subtract, ALU.mult)
                    last.then_inc(normed, 1)
                u = s - STATE_LAG
                if is_inner(u):
                    k = TURN_NO["state", u]
                    dve.wait_ge(state_hi_made, ahead(u - B + 1))
                    dve.tensor_tensor(nat_lo[:, u % B, :, :], turn_ps[k % 2][:, :].rearrange("p (t d) -> p t d", t=T),
                                      nat_hi[:, u % B, :, :].bitcast(F32), ALU.subtract).then_inc(turn_read, 1)
                k = s - (B + 1)
                if 0 <= k < T:
                    dve.wait_ge(norm2_hi_made, k + 1)
                    dve.tensor_tensor(eye_lo[:, k, :], later[:, k, :], eye_hi[:, k, :].bitcast(F32),
                                      ALU.subtract).then_inc(norm2_lo_made, 1)
                    dve.wait_ge(norm2_lo_made, k + 1)
                k = s - MIX_AT - 1
                if 0 <= k < T:
                    n = TURN_NO["mix", k]
                    dve.wait_ge(turned, n + 1)
                    dve.tensor_copy(later[:, k, :], turn_ps[n % 2][:, :]).then_inc(turn_read, 1)
                    dve.wait_ge(turn_read, n + 1)
                if k == T:
                    mix_link(dve.tensor_scalar(ident_off, ident[:, :], -1.0, 1.0, ALU.mult, ALU.add))
                    mix_link(dve.memset(ones_late, 1.0))
                    for t in range(T):
                        block_t = later[:, t, t * P:(t + 1) * P]
                        mix_link(dve.tensor_tensor(diag_junk[:, t, :], block_t, ident[:, :], ALU.mult))
                        mix_link(dve.tensor_reduce(diag_col[:, t:t + 1], diag_junk[:, t, :], AX.X, ALU.add))
                        mix_link(dve.tensor_scalar(diag_m[:, t, :], ident[:, :], diag_col[:, t:t + 1], None, ALU.mult))
                        mix_link(dve.tensor_tensor(block_t, block_t, ident_off, ALU.mult))
                    assert mix_steps[0] == MIX_READY
                if k == T + 2:
                    n = TURN_NO["diagonal", 0]
                    dve.wait_ge(turned, n + 1)
                    dve.tensor_copy(diag_row, turn_ps[n % 2][:, :]).then_inc(turn_read, 1)
                    dve.wait_ge(turn_read, n + 1)
                k = s - AFTER
                if 0 <= k < T:
                    dve.wait_ge(mix_hi_made, k + 1)
                    dve.tensor_tensor(adj_lo[:, k, :], later[:, k, :], adj_hi[:, k, :].bitcast(F32),
                                      ALU.subtract).then_inc(mix_lo_made, 1)

            run(dve, slot)

        @block.tensor
        def _(pe):
            pe.wait_ge(const_made, 8)
            pe.wait_ge(param_in, 16 * 19)
            pe.transpose(cand_ps[1][:, 0:D], raw[:, RAW_U3:RAW_U3 + D], ident[:, :])
            pe.transpose(cand_ps[1][:, D:2 * D], raw[:, RAW_U5:RAW_U5 + D], ident[:, :])
            pe.transpose(cand_ps[0][:, 3 * D:4 * D], raw2, ident[:, :])
            pe.wait_ge(prep_dve, STEP_FOLDED)
            for i in range(3):
                last = pe.transpose(cand_ps[0][:, i * D:(i + 1) * D], folded[:, i, :], ident[:, :])
            last.then_inc(w_turned, 1)
            pe.wait_ge(adj_in, 16)
            for k in range(T):
                for t in range(T):
                    last = pe.transpose(prep_ps[k][:, t * P:(t + 1) * P], rows[:, t, k:k + T * (P - 1) + 1:T], ident[:, :])
                last.then_inc(adj_turned, 1)
            pe.wait_ge(prep_dve, STEP_DIAG)
            pe.matmul(cand_ps[1][:, :], ones, flat3(diag_d), start=True, stop=True).then_inc(prep_pe, 1)
            pe.wait_ge(prep_dve, STEP_SCAN)
            pe.matmul(cand_ps[0][:, 0:1], tri, count[:, T - 1, N - 1:N], start=True, stop=True).then_inc(prep_pe, 1)
            pe.wait_ge(prep_dve, STEP_OWNER)
            pe.transpose(cand_ps[1][:, 0:P], owner, ident[:, :]).then_inc(prep_pe, 1)
            for k in range(T):
                pe.matmul(prep_ps[k][:, :], owner, count[:, k, :], start=True, stop=True).then_inc(prep_pe, 1)
            pe.wait_ge(prep_dve, STEP_CHOSEN)
            for k in range(T):
                pe.matmul(prep_ps[k][:, :], owner_t, chosen[:, k, :], start=True, stop=True).then_inc(prep_pe, 1)
            pe.wait_ge(prep_dve, STEP_PREP)

            def split_product(ps, w, parity, start, stop):
                hi, lo = agg_hi[:, parity, :], agg_lo[:, parity, :]
                pe.matmul(ps, w_hi[:, w, :], hi, start=start, stop=False, skip_group_check=True)
                pe.matmul(ps, w_lo[:, w, :], hi, start=False, stop=False, skip_group_check=True)
                return pe.matmul(ps, w_hi[:, w, :], lo, start=False, stop=stop, skip_group_check=True)

            def slot(s, ahead):
                if s < UNITS:
                    rows_ready(pe, s, ahead)
                    if s >= 2:
                        pe.wait_ge(agg_lo_made, ahead(s - 1))
                    if s == 0:
                        pe.wait_ge(prep_dve, STEP_PREP)
                    if s == B:
                        pe.wait_ge(adj_lo_made, T)
                    if s == AFTER:
                        pe.wait_ge(norm2_lo_made, T)
                    if s == AFTER + B:
                        pe.wait_ge(mix_lo_made, T)
                    m_hi, m_lo = (adj_hi, adj_lo) if is_step(s) or stage(s) == L3 else (eye_hi, eye_lo)
                    b = s % B
                    for k in range(T):
                        pe.matmul(agg_ps[s % 2][:, :], nat_hi[:, b, k, :], m_hi[:, k, :], start=(k == 0), stop=False)
                        pe.matmul(agg_ps[s % 2][:, :], nat_hi[:, b, k, :], m_lo[:, k, :], start=False, stop=False)
                        last = pe.matmul(agg_ps[s % 2][:, :], nat_lo[:, b, k, :], m_hi[:, k, :], start=False, stop=(k == T - 1))
                    last.then_inc(agg_done, 1)
                u = s - 1
                if 0 <= u < UNITS:
                    if is_step(u - 2):
                        pe.wait_ge(z_made, ahead(u - 2 - B + 1))
                    elif u >= 2:
                        pe.wait_ge(y_made, y_count(u - 2))
                if is_step(u):
                    pe.matmul(gate_ps[u % 2][:, :], w_full[:, U_GATE, :], feat[:, u % B, :], start=True, stop=False,
                              skip_group_check=True)
                    pe.wait_ge(agg_lo_made, ahead(u + 1))
                    split_product(gate_ps[u % 2][:, :], W_R, u % 2, False, True).then_inc(gate_done, 1)
                    if u - 2 >= B:
                        pe.wait_ge(cand_made, ahead(u - 2 - B + 1))
                    split_product(cand_ps[u % 2][:, :], W_H, u % 2, True, False)
                elif 0 <= u < UNITS:
                    w = {L0: W_L0, L2: W_L2, L3: W_L3}[stage(u)]
                    if stage(u) == L3:
                        pe.wait_ge(turn_read, TURN_NO["back", u - B] + 1)
                        pe.matmul(gate_ps[u % 2][:, :], w_full[:, U_SELF, :], feat[:, u % B, :], start=True, stop=False,
                                  skip_group_check=True)
                    pe.wait_ge(agg_lo_made, u + 1)
                    split_product(gate_ps[u % 2][:, :], w, u % 2, stage(u) != L3, True).then_inc(gate_done, 1)
                u = s - 2
                if is_step(u):
                    pe.wait_ge(reset_made, ahead(u - B + 1))
                    pe.matmul(cand_ps[u % 2][:, :], w_full[:, U_CAND, :], gate_r[:, u % 2, :], start=False, stop=True,
                              skip_group_check=True).then_inc(cand_done, 1)
                for kind, u in turns_at(s):
                    k = TURN_NO[kind, u]
                    if k >= 2:
                        pe.wait_ge(turn_read, ahead(k - 1))
                    to = turn_ps[k % 2]
                    if kind == "state" or kind == "result" and is_step(u):
                        pe.wait_ge(state_made, ahead(u - B + 1))
                        parts = [feat[:, u % B, t * P:(t + 1) * P] for t in range(T)]
                    elif kind == "result":
                        pe.wait_ge(y_made, y_count(u))
                        parts = [gate_r[:, u % 2, t * P:(t + 1) * P] for t in range(T)]
                    elif kind == "back":
                        pe.wait_ge(normed, count_of(NORMED, u))
                        parts = [res[:, u % B, t, :] for t in range(T)]
                    elif kind == "mix":
                        parts = [rows[:, t, u:u + T * (P - 1) + 1:T] for t in range(T)]
                    if kind == "diagonal":
                        pe.wait_ge(mix_dve, MIX_READY)
                        pe.matmul(to[:, :], ones_late, flat3(diag_m), start=True, stop=True).then_inc(turned, 1)
                        continue
                    for t in range(T):
                        last = pe.transpose(to[:, t * P:(t + 1) * P], parts[t], ident[:, :])
                    last.then_inc(turned, 1)
                u = s - 1
                if is_step(u):
                    pe.wait_ge(r_made, ahead(u - B + 1))
                    split_product(gate_ps[u % 2][:, :], W_ZR, u % 2, False, True).then_inc(z_done, 1)

            run(pe, slot)


def flat3(v):
    return v.rearrange("p a n -> p (a n)")


def y_count(u):
    return u + 1 if u < B else u - B * STEPS + 1


STEP_FOLDED = 7
STEP_WEIGHTS = STEP_FOLDED + 5
STEP_EYE = STEP_WEIGHTS + 2 * T
STEP_ROWSUM = STEP_EYE + 3
STEP_DIAG = STEP_ROWSUM + 1 + T
STEP_SCAN = STEP_DIAG + 1 + T + 4
STEP_OWNER = STEP_SCAN + 5
STEP_CHOSEN = STEP_OWNER + 1 + T
STEP_NEGMAX = STEP_CHOSEN + 3 + T + 2
STEP_PREP = STEP_NEGMAX + 1 + T
PE_DROW, PE_BEFORE, PE_OWNER, PE_CHOSEN = 1, 2, 3, 4
PE_VALUE = PE_CHOSEN + T
MIX_READY = 2 + 4 * T

_INS = ['x', 'adj', 'L0_gnn_weight', 'L0_gnn_bias', 'L1_gnn_w3_w', 'L1_gnn_w3_b', 'L1_gnn_u3_w', 'L1_gnn_u3_b',
        'L1_gnn_w4_w', 'L1_gnn_w4_b', 'L1_gnn_w5_w', 'L1_gnn_w5_b', 'L1_gnn_u5_w', 'L1_gnn_u5_b', 'L2_gnn_W',
        'L2_gnn_b', 'L3_gnn_W', 'L3_gnn_e', 'L3_gnn_bias']


def kernel(**inputs):
    import numpy as np
    import concourse.bacc as bacc
    from concourse.bass_utils import run_bass_kernel_spmd

    nc = bacc.Bacc("TRN2", target_bir_lowering=False, num_devices=1)
    arrays, args = {}, []
    for name in _INS:
        a = np.ascontiguousarray(inputs[name])
        arrays[f"in_{name}"] = a
        args.append(nc.dram_tensor(f"in_{name}", a.shape, mybir.dt.from_np(a.dtype), kind="ExternalInput").ap())
    args.append(nc.dram_tensor("out", (B, N, D), F32, kind="ExternalOutput").ap())
    graph_layers(nc, *args)
    r = run_bass_kernel_spmd(nc, [arrays], core_ids=[0])
    return r.results[0]["out"]
```

```python
from contextlib import ExitStack

import concourse.bass as bass
from concourse import mybir

P = 128
B, N, D = 16, 512, 128
T = N // P
STEPS = 5
EPS_NORM, EPS_LN = 1e-12, 1e-5
NEG = -9000000000000000.0
COUNT_CAP = 200.0
F32 = mybir.dt.float32
F32R = mybir.dt.float32r
BF16 = mybir.dt.bfloat16
I32 = mybir.dt.int32
ALU = mybir.AluOpType
ACT = mybir.ActivationFunctionType
AX = mybir.AxisListType

L0, L2, L3 = 0, STEPS + 1, STEPS + 2
UNITS = B * (STEPS + 3)
LAST = B * STEPS
AFTER = B * (STEPS + 1)
LOOP_FROM = B + 6
LOOPS = STEPS - 1
STATE_LAG = 6
SLOTS = UNITS + 7


def stage(u):
    return u // B


def is_step(u):
    return B <= u < AFTER


def is_inner(u):
    return B <= u < LAST


def turn_lag(u):
    return STATE_LAG if is_inner(u) else STATE_LAG + 1 if is_step(u) else 2


NORMED = sorted((u for u in range(UNITS) if not is_inner(u)), key=lambda u: (u + turn_lag(u), -u))
NORMED_ACT = [u for u in NORMED if stage(u) != L0]
SPLIT = [u for u in NORMED if stage(u) != L3]


def norms_at(s, lag):
    return [u for u in NORMED if u + turn_lag(u) + lag == s]


ADJ_AT = 1
BEFORE_AT = 2
OWNER_AT = 4
WEIGHTS_AT = 5
CHOSEN_AT = 6
VALUE_AT = 8
D_ROW_AT = 13
MIX_AT = AFTER + 1
DIAGONAL_AT = AFTER + 3


def turns_at(s):
    found = []
    if is_inner(s - STATE_LAG):
        found.append(("state", s - STATE_LAG))
    if ADJ_AT <= s < ADJ_AT + T:
        found.append(("adj", s - ADJ_AT))
    if MIX_AT <= s < MIX_AT + T:
        found.append(("mix", s - MIX_AT))
    found += [("result", u) for u in norms_at(s, 0) if is_step(u)]
    found += [("back", u) for u in norms_at(s, 3) if stage(u) in (L0, L2)]
    if s == BEFORE_AT:
        found.append(("before", 0))
    if s == OWNER_AT:
        found.append(("owner", 0))
    if WEIGHTS_AT <= s < WEIGHTS_AT + 2:
        found.append(("weights", s - WEIGHTS_AT))
    if CHOSEN_AT <= s < CHOSEN_AT + T:
        found.append(("chosen", s - CHOSEN_AT))
    if VALUE_AT <= s < VALUE_AT + T:
        found.append(("value", s - VALUE_AT))
    if s == D_ROW_AT:
        found.append(("d_row", 0))
    if s == DIAGONAL_AT:
        found.append(("diagonal", 0))
    return found


TURNS = [x for s in range(SLOTS) for x in turns_at(s)]
TURN_NO = {x: i for i, x in enumerate(TURNS)}


def read_by_act(turn):
    return turn[0] == "back" and stage(turn[1]) == L0


def reads(k):
    return sum(read_by_act(x) == read_by_act(TURNS[k]) for x in TURNS[:k + 1])


def nth(order, u):
    return order.index(u) + 1


def y_count(u):
    return u + 1 if u < B else u - B * STEPS + 1


def flat(v):
    return v.rearrange("p a n -> p (a n)")


def graph_layers(nc, x, adj, w0, b0, w3, b3, u3, ub3, w4, b4, w5, b5, u5, ub5, w2, b2, wl3, e, bl3, mix_dram, out):
    with ExitStack() as ctx:
        def sb(name, shape, dt=F32):
            return ctx.enter_context(nc.sbuf_tensor(name, shape, dt))

        def sem(name):
            return ctx.enter_context(nc.semaphore(name))

        def bank(name):
            return ctx.enter_context(nc.psum_tensor(name, [P, N], F32))

        res = sb("res", [P, B, T, D])
        nat_hi = sb("nat_hi", [P, B, T, D], F32R)
        nat_lo = sb("nat_lo", [P, B, T, D], F32R)
        feat = sb("feat", [P, B, N])
        adj_hi = sb("adj_hi", [P, T, N], F32R)
        adj_lo = sb("adj_lo", [P, T, N], F32R)
        eye_hi = sb("eye_hi", [P, T, N], F32R)
        eye_lo = sb("eye_lo", [P, T, N], F32R)
        later = sb("later", [P, T, N])
        with nc.sbuf_tensor("rows", [P, T, N], F32) as rows:
            pass
        with ExitStack() as again:
            def part(name, dt):
                return again.enter_context(nc.sbuf_tensor(name, [P, N], dt))
            feat_hi, feat_lo, reset_hi, reset_lo = (part(n, F32R) for n in ("feat_hi", "feat_lo", "reset_hi", "reset_lo"))
        diag_m, diag_row, _, _ = (sb(n, [P, N]) for n in ("diag_m", "diag_row", "unused0", "unused1"))
        agg_hi = sb("agg_hi", [P, 2, N], F32R)
        agg_lo = sb("agg_lo", [P, 2, N], F32R)
        gate_r = sb("gate_r", [P, 2, N])
        gate_z = sb("gate_z", [P, 2, N])
        cand = sb("cand", [P, 2, N])
        W_R, W_ZR, W_H, W_L2, U_GATE, U_CAND, W_L0, W_L3 = range(8)
        w_hi = sb("w_hi", [P, 8, D], F32R)
        w_lo = sb("w_lo", [P, 8, D], F32R)
        w_self = sb("w_self", [P, D])
        ident = sb("ident", [P, P])
        ones = sb("ones", [P, P])
        B_L0, B_R, B_Z, B_H, B_L2, B_L3 = range(6)
        bias = sb("bias", [P, 6])
        neg = sb("neg", [P, 1])
        cap = sb("cap", [P, 1])
        half = sb("half", [P, T])
        length = sb("length", [P, 4, T])
        stats = sb("stats", [P, 4, T, 6])
        mean_var = sb("mean_var", [P, 4, T, 2])
        rstd = sb("rstd", [P, 4, T])
        shift = sb("shift", [P, 4, T])
        e_last = sb("e_last", [P, 1])
        e_col = sb("e_col", [P, 1])
        row_sum, row_d, row_max, exp_sum, exp_inv, diag = (sb(n, [P, T]) for n in
                                                          ("row_sum", "row_d", "row_max", "exp_sum", "exp_inv", "diag"))
        before, upto, kcol = (sb(n, [P, 1]) for n in ("before", "upto", "kcol"))
        kcol_int = sb("kcol_int", [P, 1], I32)

        def as_bf16(a, b):
            return flat(feat[:, a:b, :]).bitcast(BF16)

        count = as_bf16(4, 6)
        mask = as_bf16(6, 8)
        late = mask
        chosen = feat[:, 8:12, :]
        mix = feat[:, 12:16, :]
        diag_d = feat[:, 10, :]
        d_row = feat[:, 11, :]
        kk_int = feat[:, 0, 0:P].bitcast(I32)
        kk = feat[:, 0, P:2 * P]
        owner = feat[:, 1, 0:P]
        tri_f = feat[:, 2, 0:P]
        tri = feat[:, 2, P:P + P // 2].bitcast(BF16)
        raw = flat(gate_z[:, :, :])
        RAW_W3, RAW_W4, RAW_W5, RAW_U3, RAW_U5 = 0, 2 * D, 4 * D, 6 * D, 7 * D
        raw0, raw2, raw_l3 = (cand[:, 0, i * D:(i + 1) * D] for i in range(3))
        bias_raw = cand[:, 0, 3 * D:3 * D + 5]
        folded = cand[:, 1, 0:3 * D].rearrange("p (a d) -> p a d", a=3)
        square_out = cand[:, 1, 3 * D:4 * D]
        owner_t = raw0
        owner_b = raw_l3[:, 0:P // 2].bitcast(BF16)

        agg_ps = [bank(f"agg_ps{i}") for i in range(2)]
        gate_ps = [bank(f"gate_ps{i}") for i in range(2)]
        cand_ps = [bank(f"cand_ps{i}") for i in range(2)]
        turn_ps = [bank(f"turn_ps{i}") for i in range(2)]
        prep_ps = agg_ps + gate_ps

        adj_in, first_in, param_in, stored = sem("adj_in"), sem("first_in"), sem("param_in"), sem("stored")
        x_in = [sem(f"x_in{b}") for b in range(B)]
        const_made, consts = sem("const_made"), 11
        chain_dve, chain_pool = sem("chain_dve"), sem("chain_pool")
        first_turned, first_copied = sem("first_turned"), sem("first_copied")
        eye_made, eye_hi_made, eye_lo_made = sem("eye_made"), sem("eye_hi_made"), sem("eye_lo_made")
        w0_hi_made, w0_lo_made = sem("w0_hi_made"), sem("w0_lo_made")
        folded_made, w_hi_made, w_lo_made = sem("folded_made"), sem("w_hi_made"), sem("w_lo_made")
        adj_hi_made = sem("adj_hi_made")
        row_sum_made, row_d_made, diag_d_made, l2_made = sem("row_sum_made"), sem("row_d_made"), sem("diag_d_made"), sem("l2_made")
        mask_made, neg_made, counted, owner_made = sem("mask_made"), sem("neg_made"), sem("counted"), sem("owner_made")
        owner_t_made, chosen_made, value_made = sem("owner_t_made"), sem("chosen_made"), sem("value_made")
        max_made, exp_made, mix_made = sem("max_made"), sem("exp_made"), sem("mix_made")
        diag_apart, diag_made, diag_m_made = sem("diag_apart"), sem("diag_made"), sem("diag_m_made")
        mix_stored, mix_loaded = sem("mix_stored"), sem("mix_loaded")
        x_hi_made, x_lo_made = sem("x_hi_made"), sem("x_lo_made")
        agg_done, agg_hi_made, agg_lo_made = sem("agg_done"), sem("agg_hi_made"), sem("agg_lo_made")
        gate_done = sem("gate_done")
        z_done, cand_done = sem("z_done"), sem("cand_done")
        feat_hi_made, feat_lo_made = sem("feat_hi_made"), sem("feat_lo_made")
        r_made, y_made = sem("r_made"), sem("y_made")
        reset_made, reset_hi_made, reset_lo_made = sem("reset_made"), sem("reset_hi_made"), sem("reset_lo_made")
        z_made, cand_made = sem("z_made"), sem("cand_made")
        diff_made, move_made, state_made = sem("diff_made"), sem("move_made"), sem("state_made")
        turned, by_rows = sem("turned"), sem("by_rows")
        turn_read, turn_read_act, rows_read = sem("turn_read"), sem("turn_read_act"), sem("rows_read")
        state_hi_made = sem("state_hi_made")
        squared, length_made = sem("squared"), sem("length_made")
        added, statted, stats_made, rstd_made = sem("added"), sem("statted"), sem("stats_made"), sem("rstd_made")
        normed, normed_act = sem("normed"), sem("normed_act")
        split_hi_made, split_lo_made = sem("split_hi_made"), sem("split_lo_made")
        l2_hi_made, l2_lo_made, mix_hi_made = sem("l2_hi_made"), sem("l2_lo_made"), sem("mix_hi_made")

        def wait_normed(eng, u):
            if stage(u) == L0:
                eng.wait_ge(normed, u + 1)
            else:
                eng.wait_ge(normed_act, nth(NORMED_ACT, u))

        def run(eng, slot):
            for s in range(LOOP_FROM):
                slot(s, lambda v: v)
            with eng.Fori(0, LOOPS * B, B) as done:
                for s in range(LOOP_FROM, LOOP_FROM + B):
                    slot(s, lambda v: v + done)
            for s in range(LOOP_FROM + LOOPS * B, SLOTS):
                slot(s, lambda v: v)

        block = ctx.enter_context(nc.Block())

        @block.sync
        def _(sp):
            def col(v):
                return v.rearrange("(d o) -> d o", o=1)

            def load_x(b):
                sp.dma_start(res[:, b, :, :], x[b].rearrange("(p t) d -> p t d", t=T)).then_inc(x_in[b], 16)

            sp.dma_start(rows[:, :, :], adj.rearrange("(p t) m -> p t m", t=T)).then_inc(adj_in, 16)
            load_x(0)
            sp.dma_start(raw0, w0).then_inc(first_in, 16)
            sp.dma_start(bias[:, B_L0:B_L0 + 1], col(b0)).then_inc(first_in, 16)
            for b in range(1, 4):
                load_x(b)
            for src, at in ((w3, RAW_W3), (w4, RAW_W4), (w5, RAW_W5)):
                sp.dma_start(raw[:, at:at + 2 * D], src).then_inc(param_in, 16)
            sp.dma_start(raw[:, RAW_U3:RAW_U3 + D], u3).then_inc(param_in, 16)
            sp.dma_start(raw[:, RAW_U5:RAW_U5 + D], u5).then_inc(param_in, 16)
            load_x(4)
            sp.dma_start(raw2, w2).then_inc(param_in, 16)
            sp.dma_start(w_self[:, :], wl3[0]).then_inc(param_in, 16)
            sp.dma_start(raw_l3, wl3[1]).then_inc(param_in, 16)
            sp.dma_start(bias[:, B_L2:B_L2 + 1], col(b2)).then_inc(param_in, 16)
            sp.dma_start(bias[:, B_L3:B_L3 + 1], col(bl3)).then_inc(param_in, 16)
            for i, v in enumerate((b3, b4, b5, ub3, ub5)):
                sp.dma_start(bias_raw[:, i:i + 1], col(v)).then_inc(param_in, 16)
            sp.dma_start(e_col[:, :], e.rearrange("o k -> k o")).then_inc(param_in, 16)
            sp.dma_start(e_last[:, :], e[0:1, P - 1:P].to_broadcast([P, 1])).then_inc(param_in, 16)
            for b in range(5, B):
                load_x(b)
            sp.wait_ge(diag_apart, 2)
            sp.dma_start(mix_dram.rearrange("(p t) m -> p t m", t=T), mix).then_inc(mix_stored, 16)
            sp.wait_ge(mix_stored, 16)
            sp.wait_ge(l2_lo_made, T)
            sp.dma_start(later[:, :, :], mix_dram.rearrange("(p t) m -> p t m", t=T)).then_inc(mix_loaded, 16)
            for u in range(UNITS - B, UNITS):
                wait_normed(sp, u)
                sp.dma_start(out[u % B].rearrange("(p t) d -> p t d", t=T), res[:, u % B, :, :]).then_inc(stored, 16)
            sp.wait_ge(stored, 16 * B)

        PARAMS = 16 * 17

        @block.scalar
        def _(act):
            for k in range(T):
                act.wait_ge(first_turned, k + 1)
                act.activation(later[:, k, :], prep_ps[k][:, :], ACT.Copy).then_inc(first_copied, 1)
                if k:
                    act.wait_ge(eye_made, k)
                    act.activation(eye_hi[:, k - 1, :], later[:, k - 1, :], ACT.Copy).then_inc(eye_hi_made, 1)
            act.wait_ge(x_in[0], 16)
            act.activation(nat_hi[:, 0, :, :], res[:, 0, :, :], ACT.Copy).then_inc(x_hi_made, 1)
            act.wait_ge(eye_made, T)
            act.activation(eye_hi[:, T - 1, :], later[:, T - 1, :], ACT.Copy).then_inc(eye_hi_made, 1)
            act.wait_ge(first_in, 32)
            act.activation(w_hi[:, W_L0, :], raw0, ACT.Copy).then_inc(w0_hi_made, 1)
            for b in range(1, 3):
                act.wait_ge(x_in[b], 16)
                act.activation(nat_hi[:, b, :, :], res[:, b, :, :], ACT.Copy).then_inc(x_hi_made, 1)

            def slot(s, ahead):
                u = s - 2
                if is_step(u):
                    act.wait_ge(z_done, ahead(u - B + 1))
                    if u >= B + 2:
                        act.wait_ge(move_made, ahead(u - B - 1))
                    act.activation(gate_z[:, u % 2, :], gate_ps[u % 2][:, :], ACT.Sigmoid,
                                   bias=bias[:, B_Z:B_Z + 1]).then_inc(z_made, 1)
                for n in norms_at(s, 3):
                    if stage(n) != L3:
                        if stage(n) == L0:
                            act.wait_ge(normed, n + 1)
                        else:
                            act.wait_ge(normed_act, nth(NORMED_ACT, n))
                        act.activation(nat_hi[:, n % B, :, :], res[:, n % B, :, :], ACT.Copy).then_inc(split_hi_made, 1)
                for n in norms_at(s, 4):
                    if stage(n) == L0:
                        k = TURN_NO["back", n]
                        act.wait_ge(turned, k + 1)
                        if n in (4, 6, 8, 10, 12):
                            act.wait_ge(turned, TURN_NO["chosen", T - 1] + 1)
                        if n == 6:
                            act.wait_ge(value_made, T)
                        if n == 8:
                            act.wait_ge(turned, TURN_NO["value", T - 1] + 1)
                        if n == 10:
                            act.wait_ge(l2_made, 1)
                        if n == 12:
                            act.wait_ge(mix_stored, 16)
                        act.activation(feat[:, n, :], turn_ps[k % 2][:, :], ACT.Copy).then_inc(turn_read_act, 1)
                for n in norms_at(s, 2):
                    if stage(n) != L0:
                        i, b = NORMED.index(n), n % B
                        act.wait_ge(rstd_made, i + 1)
                        for t in range(T):
                            last = act.activation(res[:, b, t, :], res[:, b, t, :], ACT.Identity,
                                                  scale=rstd[:, i % 4, t:t + 1], bias=shift[:, i % 4, t:t + 1])
                        last.then_inc(normed_act, 1)
                if s < UNITS:
                    act.wait_ge(agg_done, ahead(s + 1))
                    if s >= 2:
                        act.wait_ge(gate_done, ahead(s - 1))
                    act.activation(agg_hi[:, s % 2, :], agg_ps[s % 2][:, :], ACT.Copy).then_inc(agg_hi_made, 1)
                u = s - 1
                if 0 <= u < UNITS:
                    act.wait_ge(gate_done, ahead(u + 1))
                    if is_step(u - 2):
                        act.wait_ge(reset_lo_made, ahead(u - 2 - B + 1))
                    elif u >= 2:
                        act.wait_ge(by_rows, y_count(u - 2))
                if is_step(u):
                    act.activation(gate_r[:, u % 2, :], gate_ps[u % 2][:, :], ACT.Sigmoid,
                                   bias=bias[:, B_R:B_R + 1]).then_inc(r_made, 1)
                elif 0 <= u < UNITS:
                    at = {L0: B_L0, L2: B_L2, L3: B_L3}[stage(u)]
                    act.activation(gate_r[:, u % 2, :], gate_ps[u % 2][:, :], ACT.Identity,
                                   bias=bias[:, at:at + 1]).then_inc(y_made, 1)
                if is_step(s):
                    if s == B:
                        act.wait_ge(diag_apart, 2)
                        act.wait_ge(diag_made, 1)
                    if s > B:
                        act.wait_ge(gate_done, ahead(s))
                    act.wait_ge(turn_read_act, min(s - B + 1, B) if s < 2 * B else B)
                    if s >= 2 * B:
                        act.wait_ge(state_made, ahead(s - 2 * B + 1))
                    act.activation(feat_hi[:, :], feat[:, s % B, :], ACT.Copy).then_inc(feat_hi_made, 1)
                u = s - 2
                if is_step(u):
                    act.wait_ge(cand_done, ahead(u - B + 1))
                    if u >= B + 2:
                        act.wait_ge(state_made, ahead(u - B - 1))
                    act.activation(cand[:, u % 2, :], cand_ps[u % 2][:, :], ACT.Tanh,
                                   bias=bias[:, B_H:B_H + 1]).then_inc(cand_made, 1)
                u = s - 1
                if is_step(u):
                    act.wait_ge(reset_made, ahead(u - B + 1))
                    if u > B:
                        act.wait_ge(cand_done, ahead(u - B))
                    act.activation(reset_hi[:, :], gate_r[:, u % 2, :], ACT.Copy).then_inc(reset_hi_made, 1)
                u = s - STATE_LAG
                if is_inner(u):
                    k = TURN_NO["state", u]
                    act.wait_ge(turned, ahead(k + 1))
                    act.wait_ge(agg_done, ahead(u + 1))
                    act.activation(nat_hi[:, u % B, :, :], turn_ps[k % 2][:, :].rearrange("p (t d) -> p t d", t=T),
                                   ACT.Copy).then_inc(state_hi_made, 1)
                for n in norms_at(s, 0):
                    if stage(n) == L0:
                        act.wait_ge(by_rows, n + 1)
                        for t in range(T):
                            if n or t:
                                act.wait_ge(squared, T * n + t)
                            act.activation(square_out, cand_ps[n % 2][:, t * D:(t + 1) * D], ACT.Square,
                                           accum_out=length[:, n % 4, t:t + 1]).then_inc(squared, 1)
                if s + 3 < B:
                    act.wait_ge(x_in[s + 3], 16)
                    act.activation(nat_hi[:, s + 3, :, :], res[:, s + 3, :, :], ACT.Copy).then_inc(x_hi_made, 1)
                k = s - ADJ_AT
                if 0 <= k < T:
                    n = TURN_NO["adj", k]
                    act.wait_ge(turned, n + 1)
                    act.activation(adj_hi[:, k, :], turn_ps[n % 2][:, :], ACT.Copy).then_inc(adj_hi_made, 1)
                if s == 1:
                    act.wait_ge(mask_made, 1)
                    act.activation(flat(mix), mask, ACT.Identity, scale=-NEG, bias=neg[:, 0:1]).then_inc(neg_made, 1)
                k = s - WEIGHTS_AT
                if 0 <= k < 2:
                    n = TURN_NO["weights", k]
                    act.wait_ge(turned, n + 1)
                    w = slice(0, 4) if k == 0 else slice(4, 6)
                    cols = 4 * D if k == 0 else 2 * D
                    if k == 0:
                        act.activation(w_hi[:, W_L3, :], raw_l3, ACT.Copy).then_inc(w_hi_made, 1)
                    act.activation(w_hi[:, w, :], turn_ps[n % 2][:, 0:cols].rearrange("p (a d) -> p a d", d=D),
                                   ACT.Copy).then_inc(w_hi_made, 1)
                if s == VALUE_AT + T + 1:
                    act.wait_ge(max_made, 1)
                    for t in range(T):
                        last = act.activation(mix[:, t, :], mix[:, t, :], ACT.Exp, bias=row_max[:, t:t + 1],
                                              accum_out=exp_sum[:, t:t + 1])
                    last.then_inc(exp_made, 1)
                k = s - (B + 1)
                if 0 <= k < T:
                    act.wait_ge(agg_done, B)
                    act.wait_ge(l2_made, 1)
                    act.activation(eye_hi[:, k, :], later[:, k, :], ACT.Copy).then_inc(l2_hi_made, 1)
                k = s - MIX_AT
                if 0 <= k < T:
                    n = TURN_NO["mix", k]
                    act.wait_ge(turned, n + 1)
                    act.wait_ge(agg_done, AFTER)
                    act.activation(adj_hi[:, k, :], turn_ps[n % 2][:, :], ACT.Copy).then_inc(mix_hi_made, 1)

            run(act, slot)

        @block.gpsimd
        def _(pool):
            steps = [0]

            def link(ins):
                steps[0] += 1
                ins.then_inc(chain_pool, 1)
                pool.wait_ge(chain_pool, steps[0])

            pool.memset(ident[:, :], 1.0).then_inc(const_made, 1)
            pool.memset(tri_f, 1.0).then_inc(const_made, 1)
            pool.wait_ge(const_made, 2)
            pool.affine_select(ident[:, :], ident[:, :], pattern=[[-1, P]], compare_op=ALU.is_equal, fill=0.0,
                               base=0, channel_multiplier=1).then_inc(const_made, 1)
            pool.affine_select(tri, tri_f, pattern=[[1, P]], compare_op=ALU.is_gt, fill=0.0,
                               base=0, channel_multiplier=-1).then_inc(const_made, 1)
            pool.memset(ones[:, :], 1.0).then_inc(const_made, 1)
            pool.memset(neg[:, :], NEG).then_inc(const_made, 1)
            pool.memset(cap[:, :], COUNT_CAP).then_inc(const_made, 1)
            pool.memset(half[:, :], -0.5).then_inc(const_made, 1)
            pool.iota(kk_int, [[1, P]], base=1, channel_multiplier=0).then_inc(const_made, 1)
            pool.iota(kcol_int[:, :], [[1, 1]], base=1, channel_multiplier=1).then_inc(const_made, 1)
            pool.memset(diag[:, :], 0.0).then_inc(const_made, 1)
            pool.wait_ge(const_made, consts)

            def x_lo(b):
                pool.wait_ge(x_hi_made, b + 1)
                pool.tensor_tensor(nat_lo[:, b, :, :], res[:, b, :, :], nat_hi[:, b, :, :].bitcast(F32),
                                   ALU.subtract).then_inc(x_lo_made, 1)

            for b in range(3):
                x_lo(b)
            for s in range(SLOTS):
                for n in norms_at(s, 0):
                    if stage(n) == L0:
                        r = length[:, n % 4, :]
                        pool.wait_ge(squared, T * (n + 1))
                        link(pool.tensor_scalar(r, r, EPS_NORM ** 2, None, ALU.max))
                        pool.tensor_tensor(r, r, half[:, :], ALU.pow).then_inc(length_made, 1)
                for n in norms_at(s, 1):
                    i = NORMED.index(n)
                    r, m = rstd[:, i % 4, :], shift[:, i % 4, :]
                    pool.wait_ge(stats_made, i + 1)
                    link(pool.tensor_scalar(r, mean_var[:, i % 4, :, 1], EPS_LN, None, ALU.add))
                    link(pool.tensor_tensor(r, r, half[:, :], ALU.pow))
                    link(pool.tensor_tensor(m, r, mean_var[:, i % 4, :, 0], ALU.mult))
                    pool.tensor_scalar(m, m, -1.0, None, ALU.mult).then_inc(rstd_made, 1)
                if s + 3 < B:
                    x_lo(s + 3)
                for n in norms_at(s, 3):
                    if stage(n) != L3:
                        pool.wait_ge(split_hi_made, nth(SPLIT, n))
                        pool.tensor_tensor(nat_lo[:, n % B, :, :], res[:, n % B, :, :],
                                           nat_hi[:, n % B, :, :].bitcast(F32), ALU.subtract).then_inc(split_lo_made, 1)
                if s == ADJ_AT + T:
                    pool.wait_ge(row_sum_made, 1)
                    pool.tensor_tensor(row_d[:, :], row_sum[:, :], half[:, :], ALU.pow).then_inc(row_d_made, 1)
                if s == VALUE_AT + T + 2:
                    pool.wait_ge(mix_made, 1)
                    node = dict(pattern=[[-1, T], [1, N]], base=0, channel_multiplier=-T)
                    pool.affine_select(rows[:, :, :], mix, compare_op=ALU.is_equal, fill=0.0, **node).then_inc(diag_apart, 1)
                    pool.affine_select(mix, mix, compare_op=ALU.not_equal, fill=0.0, **node).then_inc(diag_apart, 1)

        @block.vector
        def _(dve):
            steps = [0]

            def link(ins):
                steps[0] += 1
                ins.then_inc(chain_dve, 1)
                dve.wait_ge(chain_dve, steps[0])

            dve.wait_ge(const_made, consts)
            for k in range(T):
                diagonal = later[:, k, k * P:(k + 1) * P]
                dve.wait_ge(first_copied, k + 1)
                dve.tensor_tensor(diagonal, diagonal, ident[:, :], ALU.add).then_inc(eye_made, 1)
            for k in range(T):
                dve.wait_ge(eye_hi_made, k + 1)
                dve.tensor_tensor(eye_lo[:, k, :], later[:, k, :], eye_hi[:, k, :].bitcast(F32),
                                  ALU.subtract).then_inc(eye_lo_made, 1)
            dve.wait_ge(w0_hi_made, 1)
            dve.tensor_tensor(w_lo[:, W_L0, :], raw0, w_hi[:, W_L0, :].bitcast(F32), ALU.subtract).then_inc(w0_lo_made, 1)

            def slot(s, ahead):
                for n in norms_at(s, 2):
                    if stage(n) == L0:
                        dve.wait_ge(rstd_made, n + 1)
                        for t in range(T):
                            last = dve.tensor_scalar(res[:, n, t, :], res[:, n, t, :], mean_var[:, n % 4, t, 0:1],
                                                     rstd[:, n % 4, t:t + 1], ALU.subtract, ALU.mult)
                        last.then_inc(normed, 1)
                for n in norms_at(s, 1):
                    i, b = NORMED.index(n), n % B
                    if stage(n) == L0:
                        dve.wait_ge(length_made, n + 1)
                        for t in range(T):
                            last = dve.scalar_tensor_tensor(
                                out=res[:, b, t, :], in0=cand_ps[n % 2][:, t * D:(t + 1) * D],
                                scalar=length[:, n % 4, t:t + 1], in1=res[:, b, t, :], op0=ALU.mult, op1=ALU.add)
                        last.then_inc(rows_read, 1)
                        dve.wait_ge(rows_read, n + 1)
                    else:
                        if is_step(n):
                            k = TURN_NO["result", n]
                            dve.wait_ge(turned, k + 1)
                            ps, sem_read, count_read = turn_ps[k % 2], turn_read, reads(k)
                        else:
                            dve.wait_ge(by_rows, y_count(n))
                            ps, sem_read, count_read = cand_ps[n % 2], rows_read, y_count(n)
                        dve.tensor_tensor(res[:, b, :, :], ps[:, :].rearrange("p (t d) -> p t d", t=T),
                                          res[:, b, :, :], ALU.add).then_inc(sem_read, 1)
                        dve.wait_ge(sem_read, count_read)
                    for t in range(T):
                        last = dve.bn_stats(stats[:, i % 4, t, :], res[:, b, t, :])
                    last.then_inc(statted, 1)
                    dve.wait_ge(statted, i + 1)
                    for t in range(T):
                        last = dve.bn_aggr(mean_var[:, i % 4, t, :], stats[:, i % 4, t, :])
                    last.then_inc(stats_made, 1)

                def turn_of(*key):
                    dve.wait_ge(turned, TURN_NO[key] + 1)
                    return turn_ps[TURN_NO[key] % 2]

                for n in norms_at(s, 4):
                    if stage(n) == L2:
                        if n == AFTER:
                            dve.wait_ge(turn_read, reads(TURN_NO["diagonal", 0]))
                        dve.tensor_tensor(feat[:, n % B, :], turn_of("back", n)[:, :], diag_row[:, :],
                                          ALU.mult).then_inc(turn_read, 1)
                if s == BEFORE_AT + 1:
                    link(dve.tensor_copy(kk, kk_int))
                    link(dve.tensor_copy(kcol[:, :], kcol_int[:, :]))
                    dve.tensor_copy(before[:, :], turn_of("before", 0)[:, 0:1]).then_inc(turn_read, 1)
                    dve.wait_ge(turn_read, reads(TURN_NO["before", 0]))
                    link(dve.tensor_tensor(upto[:, :], before[:, :], count[:, T * N - 1:T * N], ALU.add))
                    link(dve.tensor_scalar(owner, kk, before[:, 0:1], None, ALU.is_gt))
                    link(dve.scalar_tensor_tensor(out=owner, in0=kk, scalar=upto[:, 0:1], in1=owner,
                                                  op0=ALU.is_le, op1=ALU.mult))
                    dve.scalar_tensor_tensor(out=count, in0=count, scalar=before[:, 0:1], in1=mask,
                                             op0=ALU.add, op1=ALU.mult).then_inc(owner_made, 1)
                    dve.wait_ge(owner_made, 1)
                if s == OWNER_AT + 1:
                    dve.tensor_copy(owner_t, turn_of("owner", 0)[:, 0:P]).then_inc(turn_read, 1)
                    dve.wait_ge(neg_made, 1)
                    dve.tensor_scalar(late, count, float(P), None, ALU.is_gt).then_inc(owner_t_made, 1)
                k = s - WEIGHTS_AT - 1
                if 0 <= k < 2:
                    ps = turn_of("weights", k)
                    w = slice(0, 4) if k == 0 else slice(4, 6)
                    cols = 4 * D if k == 0 else 2 * D
                    dve.wait_ge(w_hi_made, k + 2)
                    if k == 0:
                        dve.tensor_tensor(w_lo[:, W_L3, :], raw_l3, w_hi[:, W_L3, :].bitcast(F32),
                                          ALU.subtract).then_inc(w_lo_made, 1)
                        dve.wait_ge(w_lo_made, 1)
                        dve.tensor_copy(owner_b, owner).then_inc(w_lo_made, 1)
                    dve.tensor_tensor(w_lo[:, w, :], ps[:, 0:cols].rearrange("p (a d) -> p a d", d=D),
                                      w_hi[:, w, :].bitcast(F32), ALU.subtract).then_inc(turn_read, 1)
                k = s - CHOSEN_AT - 1
                if 0 <= k < T:
                    dve.tensor_scalar(chosen[:, k, :], turn_of("chosen", k)[:, :], kcol[:, 0:1], e_col[:, 0:1],
                                      ALU.is_equal, ALU.mult).then_inc(turn_read, 1)
                k = s - VALUE_AT - 1
                if 0 <= k < T:
                    dve.tensor_tensor(mix[:, k, :], mix[:, k, :], turn_of("value", k)[:, :], ALU.add).then_inc(turn_read, 1)
                    dve.wait_ge(turn_read, reads(TURN_NO["value", k]))
                    dve.scalar_tensor_tensor(out=mix[:, k, :], in0=late[:, k * N:(k + 1) * N], scalar=e_last[:, 0:1],
                                             in1=mix[:, k, :], op0=ALU.mult, op1=ALU.add).then_inc(value_made, 1)
                    dve.wait_ge(value_made, k + 1)
                    link(dve.tensor_reduce(row_max[:, k:k + 1], mix[:, k, :], AX.X, ALU.max))
                    if k == T - 1:
                        dve.tensor_scalar(row_max[:, :], row_max[:, :], -1.0, None, ALU.mult).then_inc(max_made, 1)
                if s == D_ROW_AT + 1:
                    dve.tensor_copy(d_row, turn_of("d_row", 0)[:, :]).then_inc(turn_read, 1)
                    dve.wait_ge(turn_read, reads(TURN_NO["d_row", 0]))
                    for k in range(T):
                        last = dve.scalar_tensor_tensor(out=later[:, k, :], in0=later[:, k, :], scalar=row_d[:, k:k + 1],
                                                        in1=d_row, op0=ALU.mult, op1=ALU.mult)
                    last.then_inc(l2_made, 1)
                if s == DIAGONAL_AT + 1:
                    dve.tensor_copy(diag_row[:, :], turn_of("diagonal", 0)[:, :]).then_inc(turn_read, 1)

                if s < UNITS:
                    dve.wait_ge(agg_hi_made, ahead(s + 1))
                    dve.tensor_tensor(agg_lo[:, s % 2, :], agg_ps[s % 2][:, :], agg_hi[:, s % 2, :].bitcast(F32),
                                      ALU.subtract).then_inc(agg_lo_made, 1)
                u = s - 1
                if is_step(u):
                    dve.wait_ge(r_made, ahead(u - B + 1))
                    dve.tensor_tensor(gate_r[:, u % 2, :], gate_r[:, u % 2, :], feat[:, u % B, :],
                                      ALU.mult).then_inc(reset_made, 1)
                if is_step(s):
                    dve.wait_ge(feat_hi_made, ahead(s - B + 1))
                    dve.tensor_tensor(feat_lo[:, :], feat[:, s % B, :], feat_hi[:, :].bitcast(F32),
                                      ALU.subtract).then_inc(feat_lo_made, 1)
                u = s - 2
                if is_step(u):
                    dve.wait_ge(cand_made, ahead(u - B + 1))
                    dve.tensor_tensor(cand[:, u % 2, :], cand[:, u % 2, :], feat[:, u % B, :],
                                      ALU.subtract).then_inc(diff_made, 1)
                u = s - 1
                if is_step(u):
                    dve.wait_ge(reset_hi_made, ahead(u - B + 1))
                    dve.tensor_tensor(reset_lo[:, :], gate_r[:, u % 2, :], reset_hi[:, :].bitcast(F32),
                                      ALU.subtract).then_inc(reset_lo_made, 1)
                u = s - 2
                if is_step(u):
                    dve.wait_ge(diff_made, ahead(u - B + 1))
                    dve.wait_ge(z_made, ahead(u - B + 1))
                    dve.tensor_tensor(cand[:, u % 2, :], cand[:, u % 2, :], gate_z[:, u % 2, :],
                                      ALU.mult).then_inc(move_made, 1)
                    dve.wait_ge(move_made, ahead(u - B + 1))
                    dve.tensor_tensor(feat[:, u % B, :], feat[:, u % B, :], cand[:, u % 2, :],
                                      ALU.add).then_inc(state_made, 1)
                u = s - STATE_LAG
                if is_inner(u):
                    dve.wait_ge(state_hi_made, ahead(u - B + 1))
                    dve.tensor_tensor(nat_lo[:, u % B, :, :],
                                      turn_ps[TURN_NO["state", u] % 2][:, :].rearrange("p (t d) -> p t d", t=T),
                                      nat_hi[:, u % B, :, :].bitcast(F32), ALU.subtract).then_inc(turn_read, 1)
                k = s - ADJ_AT
                if 0 <= k < T:
                    dve.wait_ge(adj_hi_made, k + 1)
                    dve.tensor_tensor(adj_lo[:, k, :], turn_ps[TURN_NO["adj", k] % 2][:, :],
                                      adj_hi[:, k, :].bitcast(F32), ALU.subtract).then_inc(turn_read, 1)
                k = s - MIX_AT
                if 0 <= k < T:
                    dve.wait_ge(mix_hi_made, k + 1)
                    dve.tensor_tensor(adj_lo[:, k, :], turn_ps[TURN_NO["mix", k] % 2][:, :],
                                      adj_hi[:, k, :].bitcast(F32), ALU.subtract).then_inc(turn_read, 1)

                if s == 0:
                    dve.tensor_scalar(mask, flat(rows[:, :, :]), 0.0, None, ALU.is_gt).then_inc(mask_made, 1)
                    dve.wait_ge(mask_made, 1)
                if s == 1:
                    dve.tensor_tensor_scan(count, mask, cap[:, 0:1].to_broadcast([P, T * N]), 0.0, ALU.add, ALU.min).then_inc(counted, 1)
                if s == 2:
                    link(dve.tensor_reduce(row_sum[:, :], rows[:, :, :], AX.X, ALU.add))
                    dve.tensor_scalar(row_sum[:, :], row_sum[:, :], 1.0, None, ALU.add).then_inc(row_sum_made, 1)
                if s == WEIGHTS_AT - 1:
                    dve.wait_ge(param_in, PARAMS)
                    for i, at in enumerate((RAW_W4, RAW_W3, RAW_W5)):
                        link(dve.tensor_tensor(folded[:, i, :], raw[:, at:at + D], raw[:, at + D:at + 2 * D], ALU.add))
                    for i, a, b in ((B_R, 1, 3), (B_Z, 0, 3), (B_H, 2, 4)):
                        dve.tensor_tensor(bias[:, i:i + 1], bias_raw[:, a:a + 1], bias_raw[:, b:b + 1], ALU.add)
                    dve.tensor_tensor(folded[:, 1, :], folded[:, 1, :], folded[:, 0, :], ALU.subtract).then_inc(folded_made, 1)
                if s == D_ROW_AT - 1:
                    dve.wait_ge(row_d_made, 1)
                    dve.wait_ge(turned, TURN_NO["value", T - 1] + 1)
                    for t in range(T):
                        last = dve.tensor_scalar(diag_d[:, t * P:(t + 1) * P], ident[:, :], row_d[:, t:t + 1], None, ALU.mult)
                    last.then_inc(diag_d_made, 1)
                if s == VALUE_AT + T + 1:
                    dve.wait_ge(exp_made, 1)
                    link(dve.reciprocal(exp_inv[:, :], exp_sum[:, :]))
                    for t in range(T):
                        last = dve.tensor_scalar(mix[:, t, :], mix[:, t, :], exp_inv[:, t:t + 1], None, ALU.mult)
                    last.then_inc(mix_made, 1)
                if s == B - 1:
                    dve.wait_ge(diag_apart, 1)
                    dve.tensor_reduce(diag[:, :], rows[:, :, :], AX.X, ALU.add).then_inc(diag_made, 1)
                k = s - (B + 1)
                if 0 <= k < T:
                    dve.wait_ge(l2_hi_made, k + 1)
                    dve.tensor_tensor(eye_lo[:, k, :], later[:, k, :], eye_hi[:, k, :].bitcast(F32),
                                      ALU.subtract).then_inc(l2_lo_made, 1)
                if s == DIAGONAL_AT - 1:
                    dve.wait_ge(gate_done, AFTER)
                    dve.wait_ge(cand_done, AFTER - B)
                    for t in range(T):
                        last = dve.tensor_scalar(diag_m[:, t * P:(t + 1) * P], ident[:, :], diag[:, t:t + 1], None, ALU.mult)
                    last.then_inc(diag_m_made, 1)

            run(dve, slot)

        @block.tensor
        def _(pe):
            pe.wait_ge(const_made, consts)
            pe.wait_ge(adj_in, 16)

            def turn_rows(to, m, k):
                for t in range(T):
                    last = pe.transpose(to[:, t * P:(t + 1) * P], m[:, t, k:k + T * (P - 1) + 1:T], ident[:, :])
                return last

            for k in range(T):
                turn_rows(prep_ps[k], rows, k).then_inc(first_turned, 1)

            def product(ps, w, hi, lo, start, stop):
                pe.matmul(ps, w_hi[:, w, :], hi, start=start, stop=False, skip_group_check=True)
                pe.matmul(ps, w_lo[:, w, :], hi, start=False, stop=False, skip_group_check=True)
                return pe.matmul(ps, w_hi[:, w, :], lo, start=False, stop=stop, skip_group_check=True)

            def slot(s, ahead):
                if s < UNITS:
                    if s < B:
                        pe.wait_ge(x_lo_made, s + 1)
                    elif 2 * B <= s < AFTER:
                        pe.wait_ge(turn_read, ahead(reads(TURN_NO["state", s - B])))
                    else:
                        pe.wait_ge(split_lo_made, nth(SPLIT, s - B))
                    if s >= 2:
                        pe.wait_ge(agg_lo_made, ahead(s - 1))
                    if s == 0:
                        pe.wait_ge(first_copied, T)
                        pe.wait_ge(eye_lo_made, T)
                    if s == B:
                        pe.wait_ge(turn_read, reads(TURN_NO["adj", T - 1]))
                    if s == AFTER:
                        pe.wait_ge(l2_lo_made, T)
                    if s == AFTER + B:
                        pe.wait_ge(turn_read, reads(TURN_NO["mix", T - 1]))
                    m_hi, m_lo = (adj_hi, adj_lo) if is_step(s) or stage(s) == L3 else (eye_hi, eye_lo)
                    b, ps = s % B, agg_ps[s % 2][:, :]
                    for k in range(T):
                        pe.matmul(ps, nat_hi[:, b, k, :], m_hi[:, k, :], start=(k == 0), stop=False)
                        pe.matmul(ps, nat_hi[:, b, k, :], m_lo[:, k, :], start=False, stop=False)
                        last = pe.matmul(ps, nat_lo[:, b, k, :], m_hi[:, k, :], start=False, stop=(k == T - 1))
                    last.then_inc(agg_done, 1)
                u = s - 2
                if is_step(u):
                    pe.wait_ge(reset_lo_made, ahead(u - B + 1))
                    product(cand_ps[u % 2][:, :], U_CAND, reset_hi[:, :], reset_lo[:, :], False, True).then_inc(cand_done, 1)
                u = s - 1
                if 0 <= u < UNITS:
                    if is_step(u - 2):
                        pe.wait_ge(z_made, ahead(u - 2 - B + 1))
                    elif u >= 2:
                        pe.wait_ge(y_made, y_count(u - 2))
                gate, cand_bank = gate_ps[u % 2][:, :], cand_ps[u % 2][:, :]
                parts = agg_hi[:, u % 2, :], agg_lo[:, u % 2, :]
                if is_step(u):
                    if u == B:
                        pe.wait_ge(turn_read, reads(TURN_NO["weights", 1]))
                    pe.wait_ge(feat_lo_made, ahead(u - B + 1))
                    product(gate, U_GATE, feat_hi[:, :], feat_lo[:, :], True, False)
                    pe.wait_ge(agg_lo_made, ahead(u + 1))
                    product(gate, W_R, *parts, False, True).then_inc(gate_done, 1)
                    if u >= B + 2:
                        pe.wait_ge(cand_made, ahead(u - 2 - B + 1))
                    else:
                        pe.wait_ge(rows_read, u - 2 + 1)
                    product(cand_bank, W_H, *parts, True, False)
                elif 0 <= u < UNITS:
                    w = {L0: W_L0, L2: W_L2, L3: W_L3}[stage(u)]
                    if u == 0:
                        pe.wait_ge(w0_lo_made, 1)
                    if stage(u) == L3:
                        pe.wait_ge(turn_read, reads(TURN_NO["back", u - B]))
                        pe.matmul(gate, w_self[:, :], feat[:, u % B, :], start=True, stop=False, skip_group_check=True)
                    pe.wait_ge(agg_lo_made, u + 1)
                    product(gate, w, *parts, stage(u) != L3, True).then_inc(gate_done, 1)
                u = s - 2
                if 0 <= u < UNITS and not is_step(u):
                    if is_step(u - 2):
                        pe.wait_ge(cand_made, u - 2 - B + 1)
                    elif u >= 2:
                        pe.wait_ge(rows_read, y_count(u - 2))
                    pe.wait_ge(y_made, y_count(u))
                    for t in range(T):
                        last = pe.transpose(cand_ps[u % 2][:, t * P:(t + 1) * P], gate_r[:, u % 2, t * P:(t + 1) * P],
                                            ident[:, :])
                    last.then_inc(by_rows, 1)
                for kind, i in turns_at(s):
                    k = TURN_NO[kind, i]
                    to = turn_ps[k % 2]
                    if k >= 2:
                        if read_by_act(TURNS[k - 2]):
                            pe.wait_ge(turn_read_act, reads(k - 2))
                        if k - 1 > sum(map(read_by_act, TURNS[:k - 1])):
                            pe.wait_ge(turn_read, ahead(sum(not read_by_act(x) for x in TURNS[:k - 1])))
                    if kind in ("state", "result"):
                        pe.wait_ge(state_made, ahead(i - B + 1))
                        for t in range(T):
                            last = pe.transpose(to[:, t * P:(t + 1) * P], feat[:, i % B, t * P:(t + 1) * P], ident[:, :])
                    elif kind == "back":
                        wait_normed(pe, i)
                        for t in range(T):
                            last = pe.transpose(to[:, t * P:(t + 1) * P], res[:, i % B, t, :], ident[:, :])
                    elif kind == "adj":
                        last = turn_rows(to, rows, i)
                    elif kind == "mix":
                        pe.wait_ge(mix_loaded, 16)
                        last = turn_rows(to, later, i)
                    elif kind == "before":
                        pe.wait_ge(counted, 1)
                        last = pe.matmul(to[:, 0:1], tri, count[:, T * N - 1:T * N], start=True, stop=True)
                    elif kind == "owner":
                        pe.wait_ge(owner_made, 1)
                        last = pe.transpose(to[:, 0:P], owner, ident[:, :])
                    elif kind == "weights" and i == 0:
                        pe.wait_ge(folded_made, 1)
                        for j in range(3):
                            pe.transpose(to[:, j * D:(j + 1) * D], folded[:, j, :], ident[:, :])
                        last = pe.transpose(to[:, 3 * D:4 * D], raw2, ident[:, :])
                    elif kind == "weights":
                        pe.transpose(to[:, 0:D], raw[:, RAW_U3:RAW_U3 + D], ident[:, :])
                        last = pe.transpose(to[:, D:2 * D], raw[:, RAW_U5:RAW_U5 + D], ident[:, :])
                    elif kind == "chosen":
                        pe.wait_ge(w_lo_made, 2)
                        last = pe.matmul(to[:, :], owner_b, count[:, i * N:(i + 1) * N], start=True, stop=True)
                    elif kind == "value":
                        pe.wait_ge(turn_read, reads(TURN_NO["chosen", i]))
                        last = pe.matmul(to[:, :], owner_t, chosen[:, i, :], start=True, stop=True)
                    elif kind == "d_row":
                        pe.wait_ge(diag_d_made, 1)
                        last = pe.matmul(to[:, :], ones[:, :], diag_d, start=True, stop=True)
                    elif kind == "diagonal":
                        pe.wait_ge(diag_m_made, 1)
                        last = pe.matmul(to[:, :], ones[:, :], diag_m[:, :], start=True, stop=True)
                    last.then_inc(turned, 1)
                u = s - 1
                if is_step(u):
                    pe.wait_ge(r_made, ahead(u - B + 1))
                    product(gate, W_ZR, *parts, False, True).then_inc(z_done, 1)

            run(pe, slot)


_INS = ['x', 'adj', 'L0_gnn_weight', 'L0_gnn_bias', 'L1_gnn_w3_w', 'L1_gnn_w3_b', 'L1_gnn_u3_w', 'L1_gnn_u3_b',
        'L1_gnn_w4_w', 'L1_gnn_w4_b', 'L1_gnn_w5_w', 'L1_gnn_w5_b', 'L1_gnn_u5_w', 'L1_gnn_u5_b', 'L2_gnn_W',
        'L2_gnn_b', 'L3_gnn_W', 'L3_gnn_e', 'L3_gnn_bias']


def kernel(**inputs):
    import numpy as np
    import concourse.bacc as bacc
    from concourse.bass_utils import run_bass_kernel_spmd

    nc = bacc.Bacc("TRN2", target_bir_lowering=False, num_devices=1)
    arrays, args = {}, []
    for name in _INS:
        a = np.ascontiguousarray(inputs[name])
        arrays[f"in_{name}"] = a
        args.append(nc.dram_tensor(f"in_{name}", a.shape, mybir.dt.from_np(a.dtype), kind="ExternalInput").ap())
    args.append(nc.dram_tensor("mix_rows", (N, N), F32, kind="Internal").ap())
    args.append(nc.dram_tensor("out", (B, N, D), F32, kind="ExternalOutput").ap())
    graph_layers(nc, *args)
    r = run_bass_kernel_spmd(nc, [arrays], core_ids=[0])
    return r.results[0]["out"]
```

```python
from contextlib import ExitStack

import concourse.bass as bass
from concourse import mybir

P = 128
B, N, D = 16, 512, 128
T = N // P
STEPS = 5
EPS_NORM, EPS_LN = 1e-12, 1e-5
NEG = -9000000000000000.0
LOWEST = -3.0e38
COUNT_CAP = 200.0
F32 = mybir.dt.float32
F32R = mybir.dt.float32r
BF16 = mybir.dt.bfloat16
I32 = mybir.dt.int32
ALU = mybir.AluOpType
ACT = mybir.ActivationFunctionType

L0, L2, L3 = 0, STEPS + 1, STEPS + 2
UNITS = B * (STEPS + 3)
LAST = B * STEPS
AFTER = B * (STEPS + 1)
LOOP_FROM = 2 * B
LOOPS = STEPS - 2
STATE_LAG = 4
LAGS = {"turn": (0, 0), "add": (1, 1), "stats": (6, 1), "shift": (7, 2), "norm": (11, 3), "split": (12, 4),
        "back": (13, 5)}
RING = 16
SLOTS = UNITS + 2 + LAGS["norm"][1] + 1


def stage(u):
    return u // B


def is_step(u):
    return B <= u < AFTER


def is_inner(u):
    return B <= u < LAST


def turn_lag(u):
    return STATE_LAG if is_step(u) else 2


NORMED = sorted((u for u in range(UNITS) if not is_inner(u)), key=lambda u: (u + turn_lag(u), -u))
SPLIT = [u for u in NORMED if stage(u) != L3]


def norms_at(s, what):
    return [u for u in NORMED if u + turn_lag(u) + LAGS[what][stage(u) != L0] == s]


def shared(n):
    return stage(n) == L0 or n == UNITS - 1 or len(norms_at(n + turn_lag(n) + LAGS["norm"][1], "norm")) == 2


SHARED = [u for u in NORMED if shared(u)]


ADJ_AT = 1
BEFORE_AT = 2
OWNER_AT = 3
CHOSEN_AT = 5
VALUE_AT = 9
WEIGHTS_AT = 13
D_ROW_AT = B + 3
SUM_AT = 3
LATE_AT = 4
EXP_AT = VALUE_AT + 1
EYE_AT = B
L2_ROWS_AT = D_ROW_AT + 1
MIX_MADE_AT = B + 4
W_SELF_AT = 2 * B - 1
L2_AT = L2_ROWS_AT + 6
MIX_AT = AFTER + 9
DIAGONAL_AT = AFTER + 4


def turns_at(s):
    found = []
    if is_inner(s - STATE_LAG):
        found.append(("state", s - STATE_LAG))
    if ADJ_AT <= s < ADJ_AT + T:
        found.append(("adj", s - ADJ_AT))
    if MIX_AT <= s < MIX_AT + T:
        found.append(("mix", s - MIX_AT))
    found += [("back", u) for u in norms_at(s, "split") if stage(u) in (L0, L2)]
    if s == BEFORE_AT:
        found.append(("before", 0))
    if s == OWNER_AT:
        found.append(("owner", 0))
    if WEIGHTS_AT <= s < WEIGHTS_AT + 2:
        found.append(("weights", s - WEIGHTS_AT))
    if CHOSEN_AT <= s < CHOSEN_AT + T:
        found.append(("chosen", s - CHOSEN_AT))
    if VALUE_AT <= s < VALUE_AT + T:
        found.append(("value", s - VALUE_AT))
    if s == D_ROW_AT:
        found.append(("d_row", 0))
    if s == DIAGONAL_AT:
        found.append(("diagonal", 0))
    found += [("result", u) for u in norms_at(s, "turn") if is_step(u)]
    return found


TURNS = [x for s in range(SLOTS) for x in turns_at(s)]
TURN_NO = {x: i for i, x in enumerate(TURNS)}


def read_by_act(turn):
    return turn[0] == "back" and stage(turn[1]) == L0


def reads(k):
    return sum(read_by_act(x) == read_by_act(TURNS[k]) for x in TURNS[:k + 1])


def nth(order, u):
    return order.index(u) + 1


def y_count(u):
    return u + 1 if u < B else u - B * STEPS + 1


def flat(v):
    return v.rearrange("p a n -> p (a n)")


def graph_layers(nc, x, adj, w0, b0, w3, b3, u3, ub3, w4, b4, w5, b5, u5, ub5, w2, b2, wl3, e, bl3, mix_dram, out):
    with ExitStack() as ctx:
        def sb(name, shape, dt=F32):
            return ctx.enter_context(nc.sbuf_tensor(name, shape, dt))

        def sem(name):
            return ctx.enter_context(nc.semaphore(name))

        def bank(name):
            return ctx.enter_context(nc.psum_tensor(name, [P, N], F32))

        res = sb("res", [P, B, T, D])
        nat_hi = sb("nat_hi", [P, B, T, D], F32R)
        nat_lo = sb("nat_lo", [P, B, T, D], F32R)
        feat = sb("feat", [P, B, N])
        adj_hi = sb("adj_hi", [P, T, N], F32R)
        adj_lo = sb("adj_lo", [P, T, N], F32R)
        eye_hi = sb("eye_hi", [P, T, N], F32R)
        eye_lo = sb("eye_lo", [P, T, N], F32R)
        later = sb("later", [P, T, N])
        with nc.sbuf_tensor("rows", [P, T, N], F32) as rows:
            pass
        with ExitStack() as again:
            def part(name, dt):
                return again.enter_context(nc.sbuf_tensor(name, [P, N], dt))
            feat_hi, feat_lo, reset_hi, reset_lo = (part(n, F32R) for n in ("feat_hi", "feat_lo", "reset_hi", "reset_lo"))
        diag_m, diag_row = (sb(n, [P, N]) for n in ("diag_m", "diag_row"))
        self_hi, self_lo = (sb(n, [P, N], F32R) for n in ("self_hi", "self_lo"))
        agg_hi = sb("agg_hi", [P, 2, N], F32R)
        agg_lo = sb("agg_lo", [P, 2, N], F32R)
        gate_r = sb("gate_r", [P, 2, N])
        gate_z = sb("gate_z", [P, 2, N])
        cand = sb("cand", [P, 2, N])
        W_R, W_ZR, W_H, W_L2, U_GATE, U_CAND, W_L0, W_L3 = range(8)
        W_SELF = W_L0
        w_hi = sb("w_hi", [P, 8, D], F32R)
        w_lo = sb("w_lo", [P, 8, D], F32R)
        w_self = sb("w_self", [P, D])
        ident = sb("ident", [P, P])
        ones = sb("ones", [P, P])
        B_L0, B_R, B_Z, B_H, B_L2, B_L3 = range(6)
        bias = sb("bias", [P, 6])
        neg = sb("neg", [P, 1])
        cap = sb("cap", [P, 1])
        half = sb("half", [P, T])
        length = sb("length", [P, 4, T])
        stats = sb("stats", [P, 4, T, 6])
        mean_var = sb("mean_var", [P, RING, T, 2])
        rstd = sb("rstd", [P, RING, T])
        shift = sb("shift", [P, RING, T])
        e_last = sb("e_last", [P, 1])
        e_col = sb("e_col", [P, 1])
        row_sum, row_d, row_max, exp_sum, exp_inv, diag = (sb(n, [P, T]) for n in
                                                          ("row_sum", "row_d", "row_max", "exp_sum", "exp_inv", "diag"))
        before, upto, kcol = (sb(n, [P, 1]) for n in ("before", "upto", "kcol"))
        kcol_int = sb("kcol_int", [P, 1], I32)

        def as_bf16(a, b):
            return flat(feat[:, a:b, :]).bitcast(BF16)

        count = as_bf16(4, 6)
        mask = as_bf16(6, 8)
        late = mask
        chosen = feat[:, 8:12, :]
        mix = feat[:, 12:16, :]
        diag_d = feat[:, 10, :]
        d_row = feat[:, 11, :]
        kk_int = feat[:, 0, 0:P].bitcast(I32)
        kk = feat[:, 0, P:2 * P]
        owner = feat[:, 1, 0:P]
        tri = feat[:, 2, P:P + P // 2].bitcast(BF16)
        raw = flat(gate_z[:, :, :])
        RAW_W3, RAW_W4, RAW_W5, RAW_U3, RAW_U5 = 0, 2 * D, 4 * D, 6 * D, 7 * D
        raw0, raw_l3, raw2 = (cand[:, 0, i * D:(i + 1) * D] for i in range(3))
        bias_raw = cand[:, 0, 3 * D:3 * D + 5]
        folded = cand[:, 1, 0:3 * D].rearrange("p (a d) -> p a d", a=3)
        square_out = cand[:, 1, 3 * D:4 * D]
        owner_t = raw0
        owner_b = raw_l3[:, 0:P // 2].bitcast(BF16)

        agg_ps = [bank(f"agg_ps{i}") for i in range(2)]
        gate_ps = [bank(f"gate_ps{i}") for i in range(2)]
        cand_ps = [bank(f"cand_ps{i}") for i in range(2)]
        turn_ps = [bank(f"turn_ps{i}") for i in range(2)]
        prep_ps = agg_ps + gate_ps

        first_in, param_in, stored = sem("first_in"), sem("param_in"), sem("stored")
        adj_in = [sem(f"adj_in{t}") for t in range(T)]
        x_in = [sem(f"x_in{b}") for b in range(B)]
        const_made, consts = sem("const_made"), 6
        chain_dve, chain_pool = sem("chain_dve"), sem("chain_pool")
        ident_made, eye_turned = sem("ident_made"), sem("eye_turned")
        eye_hi_made, eye_lo_made, eye_made = sem("eye_hi_made"), sem("eye_lo_made"), sem("eye_made")
        w0_hi_made, w0_lo_made = sem("w0_hi_made"), sem("w0_lo_made")
        folded_made, w_hi_made = sem("folded_made"), sem("w_hi_made")
        adj_hi_made = sem("adj_hi_made")
        row_sum_made, row_d_made, diag_d_made, l2_made = sem("row_sum_made"), sem("row_d_made"), sem("diag_d_made"), sem("l2_made")
        mask_made, neg_made, counted, owner_made = sem("mask_made"), sem("neg_made"), sem("counted"), sem("owner_made")
        owner_t_made, late_added = sem("owner_t_made"), sem("late_added")
        max_made, exp_made, mix_made = sem("max_made"), sem("exp_made"), sem("mix_made")
        count_made, diag_apart, diag_in, diag_m_made = sem("count_made"), sem("diag_apart"), sem("diag_in"), sem("diag_m_made")
        mix_stored, mix_loaded = sem("mix_stored"), sem("mix_loaded")
        x_hi_made, x_lo_first, x_lo_rest = sem("x_hi_made"), sem("x_lo_first"), sem("x_lo_rest")
        agg_done, agg_hi_made, agg_lo_made = sem("agg_done"), sem("agg_hi_made"), sem("agg_lo_made")
        gate_done = sem("gate_done")
        z_done, cand_done = sem("z_done"), sem("cand_done")
        feat_hi_made, feat_lo_made = sem("feat_hi_made"), sem("feat_lo_made")
        r_made, y_made = sem("r_made"), sem("y_made")
        reset_made, reset_hi_made, reset_lo_made = sem("reset_made"), sem("reset_hi_made"), sem("reset_lo_made")
        z_made, cand_made = sem("z_made"), sem("cand_made")
        diff_made, move_made, state_made = sem("diff_made"), sem("move_made"), sem("state_made")
        turned, by_rows = sem("turned"), sem("by_rows")
        turn_read, turn_read_act, rows_read = sem("turn_read"), sem("turn_read_act"), sem("rows_read")
        state_hi_made = sem("state_hi_made")
        squared, length_made, shift_made = sem("squared"), sem("length_made"), sem("shift_made")
        statted, aggregated = sem("statted"), sem("aggregated")
        stats_made, rstd_made = sem("stats_made"), sem("rstd_made")
        normed, normed_act = sem("normed"), sem("normed_act")
        split_hi_made, split_lo_made = sem("split_hi_made"), sem("split_lo_made")
        self_hi_made, self_lo_made = sem("self_hi_made"), sem("self_lo_made")
        w_self_hi_made, w_self_lo_made = sem("w_self_hi_made"), sem("w_self_lo_made")
        l2_hi_made, l2_lo_made, mix_hi_made = sem("l2_hi_made"), sem("l2_lo_made"), sem("mix_hi_made")

        def wait_normed(eng, u):
            if shared(u):
                eng.wait_ge(normed, nth(SHARED, u))
            eng.wait_ge(normed_act, nth(NORMED, u))

        def run(eng, slot):
            for s in range(LOOP_FROM):
                slot(s, lambda v: v)
            with eng.Fori(0, LOOPS * B, B) as done:
                for s in range(LOOP_FROM, LOOP_FROM + B):
                    slot(s, lambda v: v + done)
            for s in range(LOOP_FROM + LOOPS * B, SLOTS):
                slot(s, lambda v: v)

        block = ctx.enter_context(nc.Block())

        @block.sync
        def _(sp):
            def col(v):
                return v.rearrange("(d o) -> d o", o=1)

            def load_x(b):
                sp.dma_start(res[:, b, :, :], x[b].rearrange("(p t) d -> p t d", t=T)).then_inc(x_in[b], 16)

            for t in range(T):
                sp.dma_start(rows[:, t, :], adj.rearrange("(p t) m -> t p m", t=T)[t]).then_inc(adj_in[t], 16)
            load_x(0)
            sp.dma_start(raw0, w0).then_inc(first_in, 16)
            sp.dma_start(raw_l3, wl3[1]).then_inc(first_in, 16)
            sp.dma_start(bias[:, B_L0:B_L0 + 1], col(b0)).then_inc(first_in, 16)
            for b in range(1, 4):
                load_x(b)
            for src, at in ((w3, RAW_W3), (w4, RAW_W4), (w5, RAW_W5)):
                sp.dma_start(raw[:, at:at + 2 * D], src).then_inc(param_in, 16)
            sp.dma_start(raw[:, RAW_U3:RAW_U3 + D], u3).then_inc(param_in, 16)
            sp.dma_start(raw[:, RAW_U5:RAW_U5 + D], u5).then_inc(param_in, 16)
            load_x(4)
            sp.dma_start(raw2, w2).then_inc(param_in, 16)
            sp.dma_start(w_self[:, :], wl3[0]).then_inc(param_in, 16)
            sp.dma_start(bias[:, B_L2:B_L2 + 1], col(b2)).then_inc(param_in, 16)
            sp.dma_start(bias[:, B_L3:B_L3 + 1], col(bl3)).then_inc(param_in, 16)
            for i, v in enumerate((b3, b4, b5, ub3, ub5)):
                sp.dma_start(bias_raw[:, i:i + 1], col(v)).then_inc(param_in, 16)
            sp.dma_start(e_col[:, :], e.rearrange("o k -> k o")).then_inc(param_in, 16)
            sp.dma_start(e_last[:, :], e[0:1, P - 1:P].to_broadcast([P, 1])).then_inc(param_in, 16)
            for b in range(5, B):
                load_x(b)
            sp.wait_ge(mix_made, T)
            sp.dma_start(mix_dram.rearrange("(p t) m -> p t m", t=T), mix).then_inc(mix_stored, 16)
            sp.wait_ge(mix_stored, 16)
            sp.wait_ge(l2_lo_made, T)
            sp.dma_start(later[:, :, :], mix_dram.rearrange("(p t) m -> p t m", t=T)).then_inc(mix_loaded, 16)
            sp.dma_start(diag[:, :], mix_dram.rearrange("n m -> (n m)")[0:N * N:N + 1]
                         .rearrange("(p t) -> p t", t=T), allow_slow_non_contiguous=True).then_inc(diag_in, 16)
            for u in range(UNITS - B, UNITS):
                wait_normed(sp, u)
                sp.dma_start(out[u % B].rearrange("(p t) d -> p t d", t=T), res[:, u % B, :, :]).then_inc(stored, 16)
            sp.wait_ge(stored, 16 * B)

        PARAMS = 16 * 16

        @block.scalar
        def _(act):
            act.wait_ge(x_in[0], 16)
            act.activation(nat_hi[:, 0, :, :], res[:, 0, :, :], ACT.Copy).then_inc(x_hi_made, 1)
            for k in range(T):
                act.wait_ge(eye_turned, k + 1)
                act.activation(eye_hi[:, k, :], prep_ps[k][:, :], ACT.Copy).then_inc(eye_hi_made, 1)
            act.wait_ge(first_in, 48)
            act.activation(w_hi[:, W_L0:W_L3 + 1, :], cand[:, 0, 0:2 * D].rearrange("p (a d) -> p a d", d=D),
                           ACT.Copy).then_inc(w0_hi_made, 1)
            for b in range(1, 3):
                act.wait_ge(x_in[b], 16)
                act.activation(nat_hi[:, b, :, :], res[:, b, :, :], ACT.Copy).then_inc(x_hi_made, 1)

            def norm(n, first, end):
                i = NORMED.index(n)
                act.wait_ge(rstd_made, i + 1)
                act.wait_ge(shift_made, i + 1)
                for t in range(first, end):
                    last = act.activation(res[:, n % B, t, :], res[:, n % B, t, :], ACT.Identity,
                                          scale=rstd[:, i % RING, t:t + 1], bias=shift[:, i % RING, t:t + 1])
                if end == T:
                    last.then_inc(normed_act, 1)

            def slot(s, ahead):
                u = s - 2
                if is_step(u):
                    act.wait_ge(z_done, ahead(u - B + 1))
                    if u >= B + 2:
                        act.wait_ge(move_made, ahead(u - B - 1))
                    act.activation(gate_z[:, u % 2, :], gate_ps[u % 2][:, :], ACT.Sigmoid,
                                   bias=bias[:, B_Z:B_Z + 1]).then_inc(z_made, 1)
                for n in norms_at(s, "split"):
                    if stage(n) != L3:
                        wait_normed(act, n)
                        act.activation(nat_hi[:, n % B, :, :], res[:, n % B, :, :], ACT.Copy).then_inc(split_hi_made, 1)
                for n in norms_at(s, "back"):
                    if stage(n) == L0:
                        k = TURN_NO["back", n]
                        act.wait_ge(turned, k + 1)
                        if n in (4, 6, 8, 10, 12):
                            act.wait_ge(turned, TURN_NO["chosen", T - 1] + 1)
                        if n == 6:
                            act.wait_ge(late_added, T)
                        if n == 8:
                            act.wait_ge(turned, TURN_NO["value", T - 1] + 1)
                        if n == 10:
                            act.wait_ge(l2_made, T)
                        if n == 12:
                            act.wait_ge(mix_stored, 16)
                        act.activation(feat[:, n, :], turn_ps[k % 2][:, :], ACT.Copy).then_inc(turn_read_act, 1)
                for n in norms_at(s, "norm"):
                    if stage(n) == L0:
                        norm(n, T // 2, T)
                if s < UNITS:
                    act.wait_ge(agg_done, ahead(s + 1))
                    if s >= 2:
                        act.wait_ge(gate_done, ahead(s - 1))
                    act.activation(agg_hi[:, s % 2, :], agg_ps[s % 2][:, :], ACT.Copy).then_inc(agg_hi_made, 1)
                u = s - 2
                if is_step(u):
                    act.wait_ge(cand_done, ahead(u - B + 1))
                    if u >= B + 2:
                        act.wait_ge(state_made, ahead(u - B - 1))
                    act.activation(cand[:, u % 2, :], cand_ps[u % 2][:, :], ACT.Tanh,
                                   bias=bias[:, B_H:B_H + 1]).then_inc(cand_made, 1)
                for n in norms_at(s, "norm"):
                    if not shared(n):
                        norm(n, 0, T // 2)
                u = s - 1
                if 0 <= u < UNITS:
                    act.wait_ge(gate_done, ahead(u + 1))
                    if is_step(u - 2):
                        act.wait_ge(reset_lo_made, ahead(u - 2 - B + 1))
                    elif u >= 2:
                        act.wait_ge(by_rows, y_count(u - 2))
                if is_step(u):
                    act.activation(gate_r[:, u % 2, :], gate_ps[u % 2][:, :], ACT.Sigmoid,
                                   bias=bias[:, B_R:B_R + 1]).then_inc(r_made, 1)
                elif 0 <= u < UNITS:
                    at = {L0: B_L0, L2: B_L2, L3: B_L3}[stage(u)]
                    act.activation(gate_r[:, u % 2, :], gate_ps[u % 2][:, :], ACT.Identity,
                                   bias=bias[:, at:at + 1]).then_inc(y_made, 1)
                if is_step(s):
                    if s == B:
                        act.wait_ge(turned, TURN_NO["adj", T - 1] + 1)
                    if s > B:
                        act.wait_ge(gate_done, ahead(s))
                    act.wait_ge(turn_read_act, min(s - B + 1, B) if s < 2 * B else B)
                    if s >= 2 * B:
                        act.wait_ge(state_made, ahead(s - 2 * B + 1))
                    act.activation(feat_hi[:, :], feat[:, s % B, :], ACT.Copy).then_inc(feat_hi_made, 1)
                elif UNITS - B <= s < UNITS:
                    act.wait_ge(turn_read, reads(TURN_NO["back", s - B]))
                    act.wait_ge(gate_done, s)
                    act.activation(self_hi[:, :], feat[:, s % B, :], ACT.Copy).then_inc(self_hi_made, 1)
                if s == W_SELF_AT:
                    act.activation(w_hi[:, W_SELF, :], w_self[:, :], ACT.Copy).then_inc(w_self_hi_made, 1)
                u = s - 1
                if is_step(u):
                    act.wait_ge(reset_made, ahead(u - B + 1))
                    if u > B:
                        act.wait_ge(cand_done, ahead(u - B))
                    act.activation(reset_hi[:, :], gate_r[:, u % 2, :], ACT.Copy).then_inc(reset_hi_made, 1)
                u = s - STATE_LAG
                if is_inner(u):
                    k = TURN_NO["state", u]
                    act.wait_ge(turned, ahead(k + 1))
                    act.wait_ge(agg_done, ahead(u + 1))
                    act.activation(nat_hi[:, u % B, :, :], turn_ps[k % 2][:, :].rearrange("p (t d) -> p t d", t=T),
                                   ACT.Copy).then_inc(state_hi_made, 1)
                for n in norms_at(s, "norm"):
                    if stage(n) != L0:
                        norm(n, T // 2, T)
                for n in norms_at(s, "turn"):
                    if stage(n) == L0:
                        act.wait_ge(by_rows, n + 1)
                        for t in range(T):
                            if n or t:
                                act.wait_ge(squared, T * n + t)
                            act.activation(square_out, cand_ps[n % 2][:, t * D:(t + 1) * D], ACT.Square,
                                           accum_out=length[:, n % 4, t:t + 1]).then_inc(squared, 1)
                if s + 3 < B:
                    act.wait_ge(x_in[s + 3], 16)
                    act.activation(nat_hi[:, s + 3, :, :], res[:, s + 3, :, :], ACT.Copy).then_inc(x_hi_made, 1)
                k = s - ADJ_AT
                if 0 <= k < T:
                    n = TURN_NO["adj", k]
                    act.wait_ge(turned, n + 1)
                    act.activation(adj_hi[:, k, :], turn_ps[n % 2][:, :], ACT.Copy).then_inc(adj_hi_made, 1)
                k = s - SUM_AT
                if 0 <= k < T:
                    act.wait_ge(adj_in[k], 16)
                    if k:
                        act.wait_ge(row_sum_made, k)
                    act.activation(feat[:, 3, :], rows[:, k, :], ACT.Copy, accum_out=row_sum[:, k:k + 1]).then_inc(row_sum_made, 1)
                if s == 1:
                    act.wait_ge(mask_made, T)
                    act.wait_ge(const_made, consts)
                    act.activation(flat(mix), mask, ACT.Identity, scale=-NEG, bias=neg[:, 0:1]).then_inc(neg_made, 1)
                k = s - WEIGHTS_AT
                if 0 <= k < 2:
                    n = TURN_NO["weights", k]
                    act.wait_ge(turned, n + 1)
                    w = slice(0, 4) if k == 0 else slice(4, 6)
                    cols = 4 * D if k == 0 else 2 * D
                    act.activation(w_hi[:, w, :], turn_ps[n % 2][:, 0:cols].rearrange("p (a d) -> p a d", d=D),
                                   ACT.Copy).then_inc(w_hi_made, 1)
                k = s - EXP_AT
                if 0 <= k < T:
                    act.wait_ge(max_made, k + 1)
                    act.activation(mix[:, k, :], mix[:, k, :], ACT.Exp, bias=row_max[:, k:k + 1],
                                   accum_out=exp_sum[:, k:k + 1]).then_inc(exp_made, 1)
                if s == EXP_AT + T:
                    act.activation(e_last[:, :], neg[:, :], ACT.Sigmoid)
                k = s - L2_AT
                if 0 <= k < T:
                    act.wait_ge(agg_done, B)
                    act.wait_ge(l2_made, k + 1)
                    act.activation(eye_hi[:, k, :], later[:, k, :], ACT.Copy,
                                   scale=row_d[:, k:k + 1]).then_inc(l2_hi_made, 1)
                k = s - MIX_AT
                if 0 <= k < T:
                    n = TURN_NO["mix", k]
                    act.wait_ge(turned, n + 1)
                    act.wait_ge(agg_done, AFTER)
                    act.activation(adj_hi[:, k, :], turn_ps[n % 2][:, :], ACT.Copy).then_inc(mix_hi_made, 1)

            run(act, slot)

        @block.gpsimd
        def _(pool):
            steps = [0]

            def link(ins):
                steps[0] += 1
                ins.then_inc(chain_pool, 1)
                pool.wait_ge(chain_pool, steps[0])

            link(pool.memset(ident[:, :], 1.0))
            pool.affine_select(ident[:, :], ident[:, :], pattern=[[-1, P]], compare_op=ALU.is_equal, fill=0.0,
                               base=0, channel_multiplier=1).then_inc(ident_made, 1)
            link(pool.memset(ones[:, :], 1.0))
            pool.affine_select(tri, ones[:, :], pattern=[[1, P]], compare_op=ALU.is_gt, fill=0.0,
                               base=0, channel_multiplier=-1).then_inc(const_made, 1)
            pool.memset(neg[:, :], NEG).then_inc(const_made, 1)
            pool.memset(cap[:, :], COUNT_CAP).then_inc(const_made, 1)
            pool.memset(half[:, :], -0.5).then_inc(const_made, 1)
            pool.iota(kk_int, [[1, P]], base=1, channel_multiplier=0).then_inc(const_made, 1)
            pool.iota(kcol_int[:, :], [[1, 1]], base=1, channel_multiplier=1).then_inc(const_made, 1)
            pool.wait_ge(const_made, consts)

            def x_lo(b):
                pool.wait_ge(x_hi_made, b + 1)
                pool.tensor_tensor(nat_lo[:, b, :, :], res[:, b, :, :], nat_hi[:, b, :, :].bitcast(F32),
                                   ALU.subtract).then_inc(x_lo_rest, 1)

            x_lo(2)

            def slot(s, ahead):
                u = s - 2
                if is_step(u):
                    pool.wait_ge(move_made, ahead(u - B + 1))
                    pool.tensor_tensor(feat[:, u % B, :], feat[:, u % B, :], cand[:, u % 2, :],
                                       ALU.add).then_inc(state_made, 1)
                if s + 3 < B:
                    x_lo(s + 3)
                if s == 2:
                    pool.wait_ge(param_in, PARAMS)
                    for i, at in enumerate((RAW_W4, RAW_W3, RAW_W5)):
                        link(pool.tensor_tensor(folded[:, i, :], raw[:, at:at + D], raw[:, at + D:at + 2 * D], ALU.add))
                    for i, a, b in ((B_R, 1, 3), (B_Z, 0, 3), (B_H, 2, 4)):
                        pool.tensor_tensor(bias[:, i:i + 1], bias_raw[:, a:a + 1], bias_raw[:, b:b + 1], ALU.add)
                    pool.tensor_tensor(folded[:, 1, :], folded[:, 1, :], folded[:, 0, :], ALU.subtract).then_inc(folded_made, 1)
                for n in norms_at(s, "split"):
                    if stage(n) != L3:
                        pool.wait_ge(split_hi_made, nth(SPLIT, n))
                        pool.tensor_tensor(nat_lo[:, n % B, :, :], res[:, n % B, :, :],
                                           nat_hi[:, n % B, :, :].bitcast(F32), ALU.subtract).then_inc(split_lo_made, 1)
                for n in norms_at(s, "turn"):
                    if stage(n) == L0:
                        r = length[:, n % 4, :]
                        pool.wait_ge(squared, T * (n + 1))
                        link(pool.tensor_scalar(r, r, EPS_NORM ** 2, None, ALU.max))
                        pool.tensor_tensor(r, r, half[:, :], ALU.pow).then_inc(length_made, 1)
                for n in norms_at(s, "stats"):
                    i = NORMED.index(n)
                    pool.wait_ge(stats_made, i + 1)
                    pool.tensor_tensor(rstd[:, i % RING, :], mean_var[:, i % RING, :, 1], half[:, :],
                                       ALU.pow).then_inc(rstd_made, 1)
                k = s - L2_ROWS_AT
                if 0 <= k < T:
                    pool.wait_ge(turn_read, reads(TURN_NO["d_row", 0]))
                    pool.tensor_tensor(later[:, k, :], later[:, k, :], d_row, ALU.mult).then_inc(l2_made, 1)
                k = s - EYE_AT
                if 0 <= k < T:
                    pool.wait_ge(eye_lo_made, T)
                    pool.tensor_tensor(later[:, k, :], eye_hi[:, k, :].bitcast(F32), eye_lo[:, k, :].bitcast(F32),
                                       ALU.add).then_inc(eye_made, 1)
                if s == SUM_AT + T:
                    pool.wait_ge(row_sum_made, T)
                    link(pool.tensor_scalar(row_sum[:, :], row_sum[:, :], 1.0, None, ALU.add))
                    pool.tensor_tensor(row_d[:, :], row_sum[:, :], half[:, :], ALU.pow).then_inc(row_d_made, 1)
                if s == LAST:
                    pool.wait_ge(mix_loaded, 16)
                    pool.affine_select(later[:, :, :], later[:, :, :], pattern=[[-1, T], [1, N]],
                                       compare_op=ALU.not_equal, fill=0.0, base=0,
                                       channel_multiplier=-T).then_inc(diag_apart, 1)

            run(pool, slot)

        @block.vector
        def _(dve):
            steps = [0]

            def link(ins):
                steps[0] += 1
                ins.then_inc(chain_dve, 1)
                dve.wait_ge(chain_dve, steps[0])

            def x_lo(b):
                dve.wait_ge(x_hi_made, b + 1)
                dve.tensor_tensor(nat_lo[:, b, :, :], res[:, b, :, :], nat_hi[:, b, :, :].bitcast(F32),
                                  ALU.subtract).then_inc(x_lo_first, 1)

            for t in range(T):
                dve.wait_ge(adj_in[t], 16)
                dve.tensor_scalar(mask[:, t * N:(t + 1) * N], rows[:, t, :], 0.0, None, ALU.is_gt).then_inc(mask_made, 1)
            x_lo(0)
            for k in range(T):
                dve.wait_ge(eye_hi_made, k + 1)
                dve.tensor_tensor(eye_lo[:, k, :], prep_ps[k][:, :], eye_hi[:, k, :].bitcast(F32),
                                  ALU.subtract).then_inc(eye_lo_made, 1)
            dve.wait_ge(w0_hi_made, 1)
            dve.tensor_tensor(w_lo[:, W_L0:W_L3 + 1, :], cand[:, 0, 0:2 * D].rearrange("p (a d) -> p a d", d=D),
                              w_hi[:, W_L0:W_L3 + 1, :].bitcast(F32), ALU.subtract).then_inc(w0_lo_made, 1)
            x_lo(1)

            def slot(s, ahead):
                def turn_of(*key):
                    dve.wait_ge(turned, TURN_NO[key] + 1)
                    return turn_ps[TURN_NO[key] % 2]

                for n in norms_at(s, "back"):
                    if stage(n) == L2:
                        if n == AFTER:
                            dve.wait_ge(turn_read, reads(TURN_NO["diagonal", 0]))
                        dve.tensor_tensor(feat[:, n % B, :], turn_of("back", n)[:, :], diag_row[:, :],
                                          ALU.mult).then_inc(turn_read, 1)
                if s == BEFORE_AT + 1:
                    link(dve.tensor_copy(kk, kk_int))
                    link(dve.tensor_copy(kcol[:, :], kcol_int[:, :]))
                    dve.tensor_copy(before[:, :], turn_of("before", 0)[:, 0:1]).then_inc(turn_read, 1)
                    dve.wait_ge(turn_read, reads(TURN_NO["before", 0]))
                    link(dve.tensor_tensor(upto[:, :], before[:, :], count[:, T * N - 1:T * N], ALU.add))
                    link(dve.tensor_scalar(owner, kk, before[:, 0:1], None, ALU.is_gt))
                    link(dve.scalar_tensor_tensor(out=owner, in0=kk, scalar=upto[:, 0:1], in1=owner,
                                                  op0=ALU.is_le, op1=ALU.mult))
                    dve.tensor_copy(owner_b, owner).then_inc(owner_made, 1)
                    dve.tensor_scalar(count, count, before[:, 0:1], None, ALU.add).then_inc(count_made, 1)
                    dve.wait_ge(count_made, 1)
                    dve.tensor_tensor(count, count, mask, ALU.mult).then_inc(count_made, 1)
                if s == OWNER_AT + 1:
                    dve.tensor_copy(owner_t, turn_of("owner", 0)[:, 0:P]).then_inc(turn_read, 1)
                    dve.wait_ge(neg_made, 1)
                    dve.wait_ge(count_made, 2)
                    dve.tensor_scalar(late, count, float(P), None, ALU.is_gt).then_inc(owner_t_made, 1)
                k = s - WEIGHTS_AT - 1
                if 0 <= k < 2:
                    ps = turn_of("weights", k)
                    w = slice(0, 4) if k == 0 else slice(4, 6)
                    cols = 4 * D if k == 0 else 2 * D
                    dve.wait_ge(w_hi_made, k + 1)
                    dve.tensor_tensor(w_lo[:, w, :], ps[:, 0:cols].rearrange("p (a d) -> p a d", d=D),
                                      w_hi[:, w, :].bitcast(F32), ALU.subtract).then_inc(turn_read, 1)
                k = s - CHOSEN_AT - 1
                if 0 <= k < T:
                    dve.tensor_scalar(chosen[:, k, :], turn_of("chosen", k)[:, :], kcol[:, 0:1], e_col[:, 0:1],
                                      ALU.is_equal, ALU.mult).then_inc(turn_read, 1)
                k = s - VALUE_AT - 1
                if 0 <= k < T:
                    dve.wait_ge(late_added, k + 1)
                    dve.tensor_tensor_reduce(out=mix[:, k, :], in0=mix[:, k, :], in1=turn_of("value", k)[:, :],
                                             scale=1.0, scalar=LOWEST, op0=ALU.add, op1=ALU.max,
                                             accum_out=row_max[:, k:k + 1]).then_inc(turn_read, 1)
                    dve.wait_ge(turn_read, reads(TURN_NO["value", k]))
                    dve.tensor_scalar(row_max[:, k:k + 1], row_max[:, k:k + 1], -1.0, None, ALU.mult).then_inc(max_made, 1)
                if s == D_ROW_AT + 1:
                    dve.tensor_copy(d_row, turn_of("d_row", 0)[:, :]).then_inc(turn_read, 1)
                    dve.wait_ge(turn_read, reads(TURN_NO["d_row", 0]))
                if s == DIAGONAL_AT + 1:
                    dve.tensor_copy(diag_row[:, :], turn_of("diagonal", 0)[:, :]).then_inc(turn_read, 1)

                for n in norms_at(s, "add"):
                    i, b = NORMED.index(n), n % B
                    if stage(n) == L0:
                        dve.wait_ge(length_made, n + 1)
                        for t in range(T):
                            last = dve.scalar_tensor_tensor(
                                out=res[:, b, t, :], in0=cand_ps[n % 2][:, t * D:(t + 1) * D],
                                scalar=length[:, n % 4, t:t + 1], in1=res[:, b, t, :], op0=ALU.mult, op1=ALU.add)
                        last.then_inc(rows_read, 1)
                    else:
                        if is_step(n):
                            k = TURN_NO["result", n]
                            dve.wait_ge(turned, k + 1)
                            ps, read = turn_ps[k % 2], turn_read
                        else:
                            dve.wait_ge(by_rows, y_count(n))
                            ps, read = cand_ps[n % 2], rows_read
                        dve.tensor_tensor(res[:, b, :, :], ps[:, :].rearrange("p (t d) -> p t d", t=T),
                                          res[:, b, :, :], ALU.add).then_inc(read, 1)
                for n in norms_at(s, "norm"):
                    if shared(n):
                        i = NORMED.index(n)
                        dve.wait_ge(rstd_made, i + 1)
                        for t in range(T // 2):
                            last = dve.tensor_scalar(res[:, n % B, t, :], res[:, n % B, t, :],
                                                     mean_var[:, i % RING, t, 0:1], rstd[:, i % RING, t:t + 1],
                                                     ALU.subtract, ALU.mult)
                        last.then_inc(normed, 1)
                if s < UNITS:
                    dve.wait_ge(agg_hi_made, ahead(s + 1))
                    dve.tensor_tensor(agg_lo[:, s % 2, :], agg_ps[s % 2][:, :], agg_hi[:, s % 2, :].bitcast(F32),
                                      ALU.subtract).then_inc(agg_lo_made, 1)
                u = s - 2
                if is_step(u):
                    dve.wait_ge(cand_made, ahead(u - B + 1))
                    dve.tensor_tensor(cand[:, u % 2, :], cand[:, u % 2, :], feat[:, u % B, :],
                                      ALU.subtract).then_inc(diff_made, 1)
                    dve.wait_ge(diff_made, ahead(u - B + 1))
                    dve.wait_ge(z_made, ahead(u - B + 1))
                    dve.tensor_tensor(cand[:, u % 2, :], cand[:, u % 2, :], gate_z[:, u % 2, :],
                                      ALU.mult).then_inc(move_made, 1)
                u = s - 1
                if is_step(u):
                    dve.wait_ge(r_made, ahead(u - B + 1))
                    dve.tensor_tensor(gate_r[:, u % 2, :], gate_r[:, u % 2, :], feat[:, u % B, :],
                                      ALU.mult).then_inc(reset_made, 1)
                if is_step(s):
                    dve.wait_ge(feat_hi_made, ahead(s - B + 1))
                    dve.tensor_tensor(feat_lo[:, :], feat[:, s % B, :], feat_hi[:, :].bitcast(F32),
                                      ALU.subtract).then_inc(feat_lo_made, 1)
                if s == W_SELF_AT:
                    dve.wait_ge(w_self_hi_made, 1)
                    dve.tensor_tensor(w_lo[:, W_SELF, :], w_self[:, :], w_hi[:, W_SELF, :].bitcast(F32),
                                      ALU.subtract).then_inc(w_self_lo_made, 1)
                u = s - 1
                if is_step(u):
                    dve.wait_ge(reset_hi_made, ahead(u - B + 1))
                    dve.tensor_tensor(reset_lo[:, :], gate_r[:, u % 2, :], reset_hi[:, :].bitcast(F32),
                                      ALU.subtract).then_inc(reset_lo_made, 1)
                u = s - STATE_LAG
                if is_inner(u):
                    dve.wait_ge(state_hi_made, ahead(u - B + 1))
                    dve.tensor_tensor(nat_lo[:, u % B, :, :],
                                      turn_ps[TURN_NO["state", u] % 2][:, :].rearrange("p (t d) -> p t d", t=T),
                                      nat_hi[:, u % B, :, :].bitcast(F32), ALU.subtract).then_inc(turn_read, 1)
                for n in norms_at(s, "stats"):
                    i, b = NORMED.index(n), n % B
                    if is_step(n):
                        dve.wait_ge(turn_read, reads(TURN_NO["result", n]))
                    else:
                        dve.wait_ge(rows_read, y_count(n))
                    for t in range(T):
                        last = dve.bn_stats(stats[:, i % 4, t, :], res[:, b, t, :])
                    last.then_inc(statted, 1)
                    dve.wait_ge(statted, i + 1)
                    for t in range(T):
                        last = dve.bn_aggr(mean_var[:, i % RING, t, :], stats[:, i % 4, t, :])
                    last.then_inc(aggregated, 1)
                    dve.wait_ge(aggregated, i + 1)
                    dve.tensor_scalar(mean_var[:, i % RING, :, 1], mean_var[:, i % RING, :, 1], EPS_LN, None,
                                      ALU.add).then_inc(stats_made, 1)
                if UNITS - B <= s < UNITS:
                    dve.wait_ge(self_hi_made, s - (UNITS - B) + 1)
                    dve.tensor_tensor(self_lo[:, :], feat[:, s % B, :], self_hi[:, :].bitcast(F32),
                                      ALU.subtract).then_inc(self_lo_made, 1)
                for n in norms_at(s, "shift"):
                    i = NORMED.index(n)
                    dve.wait_ge(rstd_made, i + 1)
                    dve.scalar_tensor_tensor(out=shift[:, i % RING, :], in0=mean_var[:, i % RING, :, 0], scalar=-1.0,
                                             in1=rstd[:, i % RING, :], op0=ALU.mult, op1=ALU.mult).then_inc(shift_made, 1)
                k = s - ADJ_AT
                if 0 <= k < T:
                    dve.wait_ge(adj_hi_made, k + 1)
                    dve.tensor_tensor(adj_lo[:, k, :], turn_ps[TURN_NO["adj", k] % 2][:, :],
                                      adj_hi[:, k, :].bitcast(F32), ALU.subtract).then_inc(turn_read, 1)
                k = s - MIX_AT
                if 0 <= k < T:
                    dve.wait_ge(mix_hi_made, k + 1)
                    dve.tensor_tensor(adj_lo[:, k, :], turn_ps[TURN_NO["mix", k] % 2][:, :],
                                      adj_hi[:, k, :].bitcast(F32), ALU.subtract).then_inc(turn_read, 1)

                if s == 0:
                    dve.wait_ge(const_made, consts)
                    dve.wait_ge(mask_made, T)
                    dve.tensor_tensor_scan(count, mask, cap[:, 0:1].to_broadcast([P, T * N]), 0.0, ALU.add,
                                           ALU.min).then_inc(counted, 1)
                k = s - LATE_AT
                if 0 <= k < T:
                    dve.wait_ge(owner_t_made, 1)
                    dve.scalar_tensor_tensor(out=mix[:, k, :], in0=late[:, k * N:(k + 1) * N], scalar=e_last[:, 0:1],
                                             in1=mix[:, k, :], op0=ALU.mult, op1=ALU.add).then_inc(late_added, 1)
                if s == D_ROW_AT - 1:
                    dve.wait_ge(row_d_made, 1)
                    dve.wait_ge(turned, TURN_NO["value", T - 1] + 1)
                    for t in range(T):
                        last = dve.tensor_scalar(diag_d[:, t * P:(t + 1) * P], ident[:, :], row_d[:, t:t + 1], None, ALU.mult)
                    last.then_inc(diag_d_made, 1)
                k = s - MIX_MADE_AT
                if 0 <= k < T:
                    dve.wait_ge(exp_made, k + 1)
                    link(dve.reciprocal(exp_inv[:, k:k + 1], exp_sum[:, k:k + 1]))
                    dve.tensor_scalar(mix[:, k, :], mix[:, k, :], exp_inv[:, k:k + 1], None, ALU.mult).then_inc(mix_made, 1)
                k = s - L2_AT
                if 0 <= k < T:
                    dve.wait_ge(l2_hi_made, k + 1)
                    dve.scalar_tensor_tensor(out=eye_lo[:, k, :], in0=later[:, k, :], scalar=row_d[:, k:k + 1],
                                             in1=eye_hi[:, k, :].bitcast(F32), op0=ALU.mult,
                                             op1=ALU.subtract).then_inc(l2_lo_made, 1)
                if s == DIAGONAL_AT - 1:
                    dve.wait_ge(diag_in, 16)
                    dve.wait_ge(gate_done, AFTER)
                    dve.wait_ge(cand_done, AFTER - B)
                    for t in range(T):
                        last = dve.tensor_scalar(diag_m[:, t * P:(t + 1) * P], ident[:, :], diag[:, t:t + 1], None, ALU.mult)
                    last.then_inc(diag_m_made, 1)

            run(dve, slot)

        @block.tensor
        def _(pe):
            pe.wait_ge(ident_made, 1)

            def turn_rows(to, m, k):
                for t in range(T):
                    last = pe.transpose(to[:, t * P:(t + 1) * P], m[:, t, k:k + T * (P - 1) + 1:T], ident[:, :])
                return last

            for t in range(T):
                pe.wait_ge(adj_in[t], 16)
                for k in range(T):
                    block = prep_ps[k][:, t * P:(t + 1) * P]
                    last = pe.transpose(block, rows[:, t, k:k + T * (P - 1) + 1:T], ident[:, :])
                    if k == t:
                        last = pe.matmul(block, ident[:, :], ident[:, :], start=False, stop=True,
                                         skip_group_check=True)
                    if t == T - 1:
                        last.then_inc(eye_turned, 1)

            def product(ps, w, hi, lo, start, stop):
                pe.matmul(ps, w_hi[:, w, :], hi, start=start, stop=False, skip_group_check=True)
                pe.matmul(ps, w_lo[:, w, :], hi, start=False, stop=False, skip_group_check=True)
                return pe.matmul(ps, w_hi[:, w, :], lo, start=False, stop=stop, skip_group_check=True)

            def candidate(u, ahead):
                if u >= B + 2:
                    pe.wait_ge(cand_made, ahead(u - 2 - B + 1))
                else:
                    pe.wait_ge(rows_read, u - 2 + 1)
                product(cand_ps[u % 2][:, :], W_H, agg_hi[:, u % 2, :], agg_lo[:, u % 2, :], True, False)

            def slot(s, ahead):
                if s < UNITS:
                    if s < B:
                        if s < 2:
                            pe.wait_ge(x_lo_first, s + 1)
                        else:
                            pe.wait_ge(x_lo_rest, s - 1)
                    elif 2 * B <= s < AFTER:
                        pe.wait_ge(turn_read, ahead(reads(TURN_NO["state", s - B])))
                    else:
                        pe.wait_ge(split_lo_made, nth(SPLIT, s - B))
                    if s >= 2:
                        pe.wait_ge(agg_lo_made, ahead(s - 1))
                    if s == B:
                        pe.wait_ge(turn_read, reads(TURN_NO["adj", T - 1]))
                    if s == AFTER:
                        pe.wait_ge(l2_lo_made, T)
                    if s == AFTER + B:
                        pe.wait_ge(turn_read, reads(TURN_NO["mix", T - 1]))
                    m_hi, m_lo = (adj_hi, adj_lo) if is_step(s) or stage(s) == L3 else (eye_hi, eye_lo)
                    b, ps = s % B, agg_ps[s % 2][:, :]
                    for k in range(T):
                        if s == 0:
                            pe.wait_ge(eye_lo_made, k + 1)
                        pe.matmul(ps, nat_hi[:, b, k, :], m_hi[:, k, :], start=(k == 0), stop=False)
                        pe.matmul(ps, nat_hi[:, b, k, :], m_lo[:, k, :], start=False, stop=False)
                        last = pe.matmul(ps, nat_lo[:, b, k, :], m_hi[:, k, :], start=False, stop=(k == T - 1))
                    last.then_inc(agg_done, 1)
                u = s - 2
                if is_step(u):
                    pe.wait_ge(reset_lo_made, ahead(u - B + 1))
                    product(cand_ps[u % 2][:, :], U_CAND, reset_hi[:, :], reset_lo[:, :], False, True).then_inc(cand_done, 1)
                u = s - 1
                if 0 <= u < UNITS:
                    if is_step(u - 2):
                        pe.wait_ge(z_made, ahead(u - 2 - B + 1))
                    elif u >= 2:
                        pe.wait_ge(y_made, y_count(u - 2))
                gate = gate_ps[u % 2][:, :]
                parts = agg_hi[:, u % 2, :], agg_lo[:, u % 2, :]
                if is_step(u):
                    if u == B:
                        pe.wait_ge(turn_read, reads(TURN_NO["weights", 1]))
                    pe.wait_ge(feat_lo_made, ahead(u - B + 1))
                    product(gate, U_GATE, feat_hi[:, :], feat_lo[:, :], True, False)
                    pe.wait_ge(agg_lo_made, ahead(u + 1))
                    product(gate, W_R, *parts, False, True).then_inc(gate_done, 1)
                    if u >= B + 2:
                        candidate(u, ahead)
                elif 0 <= u < UNITS:
                    w = {L0: W_L0, L2: W_L2, L3: W_L3}[stage(u)]
                    if u == 0:
                        pe.wait_ge(w0_lo_made, 1)
                    if stage(u) == L3:
                        pe.wait_ge(w_self_lo_made, 1)
                        pe.wait_ge(self_lo_made, u - (UNITS - B) + 1)
                        product(gate, W_SELF, self_hi[:, :], self_lo[:, :], True, False)
                    pe.wait_ge(agg_lo_made, u + 1)
                    product(gate, w, *parts, stage(u) != L3, True).then_inc(gate_done, 1)
                u = s - 2
                if 0 <= u < UNITS and not is_step(u):
                    if is_step(u - 2):
                        pe.wait_ge(cand_made, u - 2 - B + 1)
                    elif u >= 2:
                        pe.wait_ge(rows_read, y_count(u - 2))
                    pe.wait_ge(y_made, y_count(u))
                    for t in range(T):
                        last = pe.transpose(cand_ps[u % 2][:, t * P:(t + 1) * P], gate_r[:, u % 2, t * P:(t + 1) * P],
                                            ident[:, :])
                    last.then_inc(by_rows, 1)
                for kind, i in turns_at(s):
                    k = TURN_NO[kind, i]
                    to = turn_ps[k % 2]
                    if k >= 2:
                        if read_by_act(TURNS[k - 2]):
                            pe.wait_ge(turn_read_act, reads(k - 2))
                        if k - 1 > sum(map(read_by_act, TURNS[:k - 1])):
                            pe.wait_ge(turn_read, ahead(sum(not read_by_act(x) for x in TURNS[:k - 1])))
                    if kind in ("state", "result"):
                        pe.wait_ge(state_made, ahead(i - B + 1))
                        for t in range(T):
                            last = pe.transpose(to[:, t * P:(t + 1) * P], feat[:, i % B, t * P:(t + 1) * P], ident[:, :])
                    elif kind == "back":
                        wait_normed(pe, i)
                        for t in range(T):
                            last = pe.transpose(to[:, t * P:(t + 1) * P], res[:, i % B, t, :], ident[:, :])
                    elif kind == "adj":
                        last = turn_rows(to, rows, i)
                    elif kind == "mix":
                        pe.wait_ge(diag_apart, 1)
                        last = turn_rows(to, later, i)
                    elif kind == "before":
                        pe.wait_ge(counted, 1)
                        last = pe.matmul(to[:, 0:1], tri, count[:, T * N - 1:T * N], start=True, stop=True)
                    elif kind == "owner":
                        pe.wait_ge(owner_made, 1)
                        last = pe.transpose(to[:, 0:P], owner, ident[:, :])
                    elif kind == "weights" and i == 0:
                        pe.wait_ge(folded_made, 1)
                        for j in range(3):
                            pe.transpose(to[:, j * D:(j + 1) * D], folded[:, j, :], ident[:, :])
                        last = pe.transpose(to[:, 3 * D:4 * D], raw2, ident[:, :])
                    elif kind == "weights":
                        pe.transpose(to[:, 0:D], raw[:, RAW_U3:RAW_U3 + D], ident[:, :])
                        last = pe.transpose(to[:, D:2 * D], raw[:, RAW_U5:RAW_U5 + D], ident[:, :])
                    elif kind == "chosen":
                        pe.wait_ge(count_made, 2)
                        last = pe.matmul(to[:, :], owner_b, count[:, i * N:(i + 1) * N], start=True, stop=True)
                    elif kind == "value":
                        pe.wait_ge(turn_read, reads(TURN_NO["chosen", i]))
                        last = pe.matmul(to[:, :], owner_t, chosen[:, i, :], start=True, stop=True)
                    elif kind == "d_row":
                        pe.wait_ge(diag_d_made, 1)
                        last = pe.matmul(to[:, :], ones[:, :], diag_d, start=True, stop=True)
                    elif kind == "diagonal":
                        pe.wait_ge(diag_m_made, 1)
                        last = pe.matmul(to[:, :], ones[:, :], diag_m[:, :], start=True, stop=True)
                    last.then_inc(turned, 1)
                u = s - 1
                if B <= u < B + 2:
                    candidate(u, ahead)
                if is_step(u):
                    pe.wait_ge(r_made, ahead(u - B + 1))
                    product(gate, W_ZR, *parts, False, True).then_inc(z_done, 1)

            run(pe, slot)


_INS = ['x', 'adj', 'L0_gnn_weight', 'L0_gnn_bias', 'L1_gnn_w3_w', 'L1_gnn_w3_b', 'L1_gnn_u3_w', 'L1_gnn_u3_b',
        'L1_gnn_w4_w', 'L1_gnn_w4_b', 'L1_gnn_w5_w', 'L1_gnn_w5_b', 'L1_gnn_u5_w', 'L1_gnn_u5_b', 'L2_gnn_W',
        'L2_gnn_b', 'L3_gnn_W', 'L3_gnn_e', 'L3_gnn_bias']


def kernel(**inputs):
    import numpy as np
    import concourse.bacc as bacc
    from concourse.bass_utils import run_bass_kernel_spmd

    nc = bacc.Bacc("TRN2", target_bir_lowering=False, num_devices=1)
    arrays, args = {}, []
    for name in _INS:
        a = np.ascontiguousarray(inputs[name])
        arrays[f"in_{name}"] = a
        args.append(nc.dram_tensor(f"in_{name}", a.shape, mybir.dt.from_np(a.dtype), kind="ExternalInput").ap())
    args.append(nc.dram_tensor("mix_rows", (N, N), F32, kind="Internal").ap())
    args.append(nc.dram_tensor("out", (B, N, D), F32, kind="ExternalOutput").ap())
    graph_layers(nc, *args)
    r = run_bass_kernel_spmd(nc, [arrays], core_ids=[0])
    return r.results[0]["out"]
```
